# Optimizing a Trainium2 kernel written in Bass

```python
import numpy as np
import jax
import jax.numpy as jnp

def _softmax(x, axis=-1):
    return jax.nn.softmax(x, axis=axis)

def _gelu(x):
    return jax.nn.gelu(x, approximate=True)

def _silu(x):
    return jax.nn.silu(x)

def _sigmoid(x):
    return jax.nn.sigmoid(x)

def _layernorm(x, axis=-1, eps=1e-05):
    m = jnp.mean(x, axis=axis, keepdims=True)
    v = jnp.var(x, axis=axis, keepdims=True)
    return (x - m) / jnp.sqrt(v + eps)

def _scatter_add(tgt, idx, src, axis=0):
    return tgt.at[idx].add(src)

def _segment_sum(src, seg, n):
    return jax.ops.segment_sum(src, seg, n)
kernel_name = 'mk_prb_d1_jaxref_r4_76b4dd'

def setup_inputs(seed: int=0):
    np.random.seed(seed)
    _w = jnp.asarray

    def _L0_attn_setup():
        import jax, jax.numpy as jnp
        import numpy as np
        LORA_RANK = 16
        LORA_ALPHA = 32
        CHUNK_SIZE = 64
        TTT_LR = 0.01
        CLIP_THRESHOLD = 1.0
        SCALING = LORA_ALPHA / LORA_RANK
        LN_EPS = 1e-05

        def _forward(x, Wb, init_A, init_B, ln_gamma, ln_beta, Wp):
            B_sz, Seq, k_dim = x.shape
            h_dim = Wb.shape[0]
            r = init_A.shape[1]
            nc = Seq // CHUNK_SIZE
            base_out = x @ Wb.T
            xd = jax.lax.stop_gradient(x)
            mu = jnp.mean(xd, axis=-1, keepdims=True)
            var = jnp.mean((xd - mu) ** 2, axis=-1, keepdims=True)
            xn = (xd - mu) * jax.lax.rsqrt(var + LN_EPS) * ln_gamma + ln_beta
            shifted = jnp.pad(xn[:, 1:, :], ((0, 0), (0, 1), (0, 0)))
            shifted = jax.lax.stop_gradient(shifted)
            V = shifted @ Wp.T
            Z = x.reshape(B_sz * nc, CHUNK_SIZE, k_dim)
            Vc = V.reshape(B_sz * nc, CHUNK_SIZE, h_dim)
            proj_in = Z @ init_B.T
            dA = jnp.einsum('bch,bcr->bhr', Vc, proj_in)
            proj_err = Vc @ init_A
            dB = jnp.einsum('bcr,bck->brk', proj_err, Z)
            dA = dA.reshape(B_sz, nc, h_dim, r)
            dB = dB.reshape(B_sz, nc, r, k_dim)
            accA = jnp.cumsum(dA, axis=1)
            accB = jnp.cumsum(dB, axis=1)
            accA = jnp.concatenate([jnp.zeros_like(accA[:, :1]), accA[:, :-1]], axis=1)
            accB = jnp.concatenate([jnp.zeros_like(accB[:, :1]), accB[:, :-1]], axis=1)
            lr = TTT_LR * SCALING
            rawA = (lr * accA).reshape(-1, h_dim, r)
            rawB = (lr * accB).reshape(-1, r, k_dim)
            norm_sq = jnp.sum(rawA.astype(jnp.float32) ** 2, axis=(-2, -1), keepdims=True) + jnp.sum(rawB.astype(jnp.float32) ** 2, axis=(-2, -1), keepdims=True)
            total_norm = jnp.sqrt(norm_sq)
            coef = jnp.minimum(CLIP_THRESHOLD / (total_norm + 1e-06), 1.0).astype(rawA.dtype)
            A_eff = init_A[None] - rawA * coef
            B_eff = init_B[None] - rawB * coef
            mid = jnp.einsum('bck,brk->bcr', Z, B_eff)
            lora = jnp.einsum('bcr,bhr->bch', mid, A_eff)
            lora = lora.reshape(B_sz, Seq, h_dim)
            return base_out + lora * SCALING
        key = jax.random.key(seed)
        ks = jax.random.split(key, 5)
        B, S, K, H = (2, 2048, 256, 256)
        x = jax.random.normal(ks[0], (B, S, K), dtype=jnp.float32)
        Wb = jax.random.normal(ks[1], (H, K), dtype=jnp.float32) / np.sqrt(K)
        init_A = jax.random.normal(ks[2], (H, LORA_RANK), dtype=jnp.float32) * 0.01
        init_B = jax.random.normal(ks[3], (LORA_RANK, K), dtype=jnp.float32) * 0.01
        ln_gamma = jnp.ones((K,), dtype=jnp.float32)
        ln_beta = jnp.zeros((K,), dtype=jnp.float32)
        Wp = jax.random.normal(ks[4], (H, K), dtype=jnp.float32) / np.sqrt(K)
        return {'x': x, 'Wb': Wb, 'init_A': init_A, 'init_B': init_B, 'ln_gamma': ln_gamma, 'ln_beta': ln_beta, 'Wp': Wp}
    _L0_attn_in = _L0_attn_setup()

    def _L0_ffn_setup():
        import jax, jax.numpy as jnp
        import numpy as np
        B, K, D = (128, 32, 256)
        E = 32
        H = int(D * 0.25)

        def _rsqrt_uniform(key, shape, d):
            bound = d ** (-0.5)
            return jax.random.uniform(key, shape, jnp.float32, -bound, bound)
        key = jax.random.key(seed)
        ks = jax.random.split(key, 7)
        return {'x': jax.random.normal(ks[0], (B, K, D), jnp.float32), 'router_w': _rsqrt_uniform(ks[1], (E, D), D), 'router_b': _rsqrt_uniform(ks[2], (E,), D), 'weights1': _rsqrt_uniform(ks[3], (E, D, H), H), 'bias1': _rsqrt_uniform(ks[4], (E, H), H), 'weights2': _rsqrt_uniform(ks[5], (E, H, D), D), 'bias2': _rsqrt_uniform(ks[6], (E, D), D)}
    _L0_ffn_in = _L0_ffn_setup()
    _d = {'L0_attn_x': _L0_attn_in['x'], 'L0_attn_Wb': _L0_attn_in['Wb'], 'L0_attn_init_A': _L0_attn_in['init_A'], 'L0_attn_init_B': _L0_attn_in['init_B'], 'L0_attn_ln_gamma': _L0_attn_in['ln_gamma'], 'L0_attn_ln_beta': _L0_attn_in['ln_beta'], 'L0_attn_Wp': _L0_attn_in['Wp'], 'L0_ffn_router_w': _L0_ffn_in['router_w'], 'L0_ffn_router_b': _L0_ffn_in['router_b'], 'L0_ffn_weights1': _L0_ffn_in['weights1'], 'L0_ffn_bias1': _L0_ffn_in['bias1'], 'L0_ffn_weights2': _L0_ffn_in['weights2'], 'L0_ffn_bias2': _L0_ffn_in['bias2']}
    _x0 = _d['L0_attn_x']
    _d['L0_attn_x'] = jax.random.normal(jax.random.fold_in(jax.random.key(seed), 1), (4, 1024, 256), dtype=_x0.dtype)
    del _x0
    return _d

def reference(L0_attn_x, L0_attn_Wb, L0_attn_init_A, L0_attn_init_B, L0_attn_ln_gamma, L0_attn_ln_beta, L0_attn_Wp, L0_ffn_router_w, L0_ffn_router_b, L0_ffn_weights1, L0_ffn_bias1, L0_ffn_weights2, L0_ffn_bias2):

    def _L0_attn_ref(x, Wb, init_A, init_B, ln_gamma, ln_beta, Wp):
        import jax, jax.numpy as jnp
        import numpy as np
        LORA_RANK = 16
        LORA_ALPHA = 32
        CHUNK_SIZE = 64
        TTT_LR = 0.01
        CLIP_THRESHOLD = 1.0
        SCALING = LORA_ALPHA / LORA_RANK
        LN_EPS = 1e-05

        def _forward(x, Wb, init_A, init_B, ln_gamma, ln_beta, Wp):
            B_sz, Seq, k_dim = x.shape
            h_dim = Wb.shape[0]
            r = init_A.shape[1]
            nc = Seq // CHUNK_SIZE
            base_out = x @ Wb.T
            xd = jax.lax.stop_gradient(x)
            mu = jnp.mean(xd, axis=-1, keepdims=True)
            var = jnp.mean((xd - mu) ** 2, axis=-1, keepdims=True)
            xn = (xd - mu) * jax.lax.rsqrt(var + LN_EPS) * ln_gamma + ln_beta
            shifted = jnp.pad(xn[:, 1:, :], ((0, 0), (0, 1), (0, 0)))
            shifted = jax.lax.stop_gradient(shifted)
            V = shifted @ Wp.T
            Z = x.reshape(B_sz * nc, CHUNK_SIZE, k_dim)
            Vc = V.reshape(B_sz * nc, CHUNK_SIZE, h_dim)
            proj_in = Z @ init_B.T
            dA = jnp.einsum('bch,bcr->bhr', Vc, proj_in)
            proj_err = Vc @ init_A
            dB = jnp.einsum('bcr,bck->brk', proj_err, Z)
            dA = dA.reshape(B_sz, nc, h_dim, r)
            dB = dB.reshape(B_sz, nc, r, k_dim)
            accA = jnp.cumsum(dA, axis=1)
            accB = jnp.cumsum(dB, axis=1)
            accA = jnp.concatenate([jnp.zeros_like(accA[:, :1]), accA[:, :-1]], axis=1)
            accB = jnp.concatenate([jnp.zeros_like(accB[:, :1]), accB[:, :-1]], axis=1)
            lr = TTT_LR * SCALING
            rawA = (lr * accA).reshape(-1, h_dim, r)
            rawB = (lr * accB).reshape(-1, r, k_dim)
            norm_sq = jnp.sum(rawA.astype(jnp.float32) ** 2, axis=(-2, -1), keepdims=True) + jnp.sum(rawB.astype(jnp.float32) ** 2, axis=(-2, -1), keepdims=True)
            total_norm = jnp.sqrt(norm_sq)
            coef = jnp.minimum(CLIP_THRESHOLD / (total_norm + 1e-06), 1.0).astype(rawA.dtype)
            A_eff = init_A[None] - rawA * coef
            B_eff = init_B[None] - rawB * coef
            mid = jnp.einsum('bck,brk->bcr', Z, B_eff)
            lora = jnp.einsum('bcr,bhr->bch', mid, A_eff)
            lora = lora.reshape(B_sz, Seq, h_dim)
            return base_out + lora * SCALING
        return _forward(x, Wb, init_A, init_B, ln_gamma, ln_beta, Wp)

    def _L0_ffn_ref(x, router_w, router_b, weights1, bias1, weights2, bias2):
        import jax, jax.numpy as jnp
        import numpy as np
        B, K, D = (128, 32, 256)
        E = 32
        H = int(D * 0.25)

        def _rsqrt_uniform(key, shape, d):
            bound = d ** (-0.5)
            return jax.random.uniform(key, shape, jnp.float32, -bound, bound)
        b, k, d = x.shape
        x_flat = x.reshape(-1, d)
        n = x_flat.shape[0]
        logits = x_flat @ router_w.T + router_b
        routed_idx = jnp.argmax(logits, axis=-1)

        def expert_mlp(w1, b1, w2, b2):
            h = jax.nn.relu(x_flat @ w1 + b1)
            return jax.nn.relu(h @ w2 + b2)
        y_all = jax.vmap(expert_mlp)(weights1, bias1, weights2, bias2)
        out_flat = y_all[routed_idx, jnp.arange(n)]
        return out_flat.reshape(b, k, d)
    x = L0_attn_x
    xn = _layernorm(x, axis=-1)
    x = x + _L0_attn_ref(xn, L0_attn_Wb, L0_attn_init_A, L0_attn_init_B, L0_attn_ln_gamma, L0_attn_ln_beta, L0_attn_Wp) + _L0_ffn_ref(xn, L0_ffn_router_w, L0_ffn_router_b, L0_ffn_weights1, L0_ffn_bias1, L0_ffn_weights2, L0_ffn_bias2)
    return x

_drawn_inputs = setup_inputs


def setup_inputs(seed=0):
    import zlib

    import numpy as np

    out = dict(_drawn_inputs(seed))
    spreads = {'L0_attn_ln_gamma': (1.0, 0.6), 'L0_attn_ln_beta': (0.0, 2.0)}
    factors = {'L0_attn_init_A': 3.381,
     'L0_attn_init_B': 3.401,
     'L0_attn_Wp': 3.206,
     'L0_ffn_bias1': 8.0,
     'L0_ffn_bias2': 3.3}
    for name, (base, spread) in spreads.items():
        noise = np.random.default_rng([zlib.crc32(name.encode()), seed]).standard_normal(out[name].shape)
        drawn = base * np.exp(spread * noise) if base else spread * noise
        out[name] = jnp.asarray(drawn.astype(out[name].dtype))
    for name, factor in factors.items():
        out[name] = (out[name] * factor).astype(out[name].dtype)
    return out
```

```python
from contextlib import ExitStack

import concourse.bass as bass
from concourse import mybir
from concourse.alu_op_type import AluOpType as ALU

F32 = mybir.dt.float32
BF16 = mybir.dt.bfloat16
I32 = mybir.dt.int32
ACT = mybir.ActivationFunctionType
AX = mybir.AxisListType

P = 128
D = 256
KH = D // P
N = 4096
TILES = N // P
BATCHES = 4
TB = TILES // BATCHES
TG = TB // 2
GT = TG * P
R = 16
CHUNK = 64
CB = TB * P // CHUNK
CG = CB // 2
E = 32
H = 64
ITEMS = 64
CREDIT = 1
CLEARED = 11
RING = 4
LR = 0.01 * 2.0
SCALING = 2.0
EPS = 1e-5
PK = 1 << 12

EARLY = [("ident", P), ("w64", KH * 64), ("rb", E), ("edesc", E), ("wp", KH * D), ("a", KH * R), ("gb", KH * 2)]
LATE = [("eiota", E), ("icol", 1), ("ones", P), ("ntri", P), ("sh", 6 * P), ("blk", P), ("diag", GT),
        ("wpt", KH * D), ("wbt", KH * D), ("atrep", D), ("btrep", KH * P)]


class Count:

    def __init__(self, at):
        self.at, self.k = at, 0

    def __call__(self, k=1):
        self.k += k
        return self.at + self.k


def build(nc, x, early, late, w1p, w2p, out):
    ctx = ExitStack()
    with ctx:
        def sb(name, shape, dt=F32):
            return ctx.enter_context(nc.sbuf_tensor(name, shape, dt))

        def sem(name):
            return ctx.enter_context(nc.semaphore(name))

        def pair(name):
            return [sem(f"{name}{h}") for h in range(2)]

        xs_dram = nc.dram_tensor("xs_dram", [N, D], F32, kind="Internal").ap()
        y_dram = nc.dram_tensor("y_dram", [ITEMS * P, D], F32, kind="Internal").ap()

        e_sb = sb("e_sb", [P, sum(w for _, w in EARLY)])
        l_sb = sb("l_sb", [P, sum(w for _, w in LATE)])
        col = {}
        for t, names in ((e_sb, EARLY), (l_sb, LATE)):
            at = 0
            for n, w in names:
                col[n] = t[:, at:at + w]
                at += w
        ident, edesc, eiota, icol, ones, blk, diag = (col[k] for k in ("ident", "edesc", "eiota", "icol", "ones", "blk", "diag"))
        w64 = col["w64"].rearrange("p (k c) -> p k c", k=KH)
        wp = col["wp"].rearrange("p (k d) -> p k d", k=KH)
        a_w = col["a"].rearrange("p (k r) -> p k r", k=KH)
        gb = col["gb"].rearrange("p (k c) -> p k c", k=KH)
        wpt = col["wpt"].rearrange("p (k h) -> p k h", k=KH)
        wbt = col["wbt"].rearrange("p (k h) -> p k h", k=KH)
        btrep = col["btrep"].rearrange("p (k c) -> p k c", k=KH)
        shift = [col["sh"][:, i * P:(i + 1) * P] for i in range(6)]

        wpgt = sb("wpgt", [P, KH, D])
        gbn = sb("gbn", [P, KH, 2])
        ws = sb("ws", [2, D])
        bwa = sb("bwa", [P, KH, R])
        g1b1 = sb("g1b1", [P, 2, R])
        at2 = sb("at2", [P, D])
        ones_bf = sb("ones_bf", [P, P], BF16)
        ntri_bf = sb("ntri_bf", [P, P], BF16)
        reset = sb("reset", [P, E, TILES])
        reset2 = sb("reset2", [P, KH * 2 * R, CB])

        x_all = sb("x_all", [P, TILES, D])
        xn_all = sb("xn_all", [P, TILES, D])
        xt_all = sb("xt_all", [P, TILES // TG, KH, GT])
        xst = sb("xst", [P, KH, N + P])
        shared = xst[:].rearrange("p k n -> p (k n)")
        used = [0]

        def before_xst(shape):
            size = 1
            for w in shape[1:]:
                size *= w
            view = shared[0:shape[0], used[0]:used[0] + size]
            used[0] += size
            assert used[0] <= KH * (N + P)
            names = "abcd"[:len(shape) - 1]
            return view.rearrange(f"p ({' '.join(names)}) -> p {' '.join(names)}", **dict(zip(names, shape[1:])))

        ep_all = sb("ep_all", [P, TILES, 2 * R])
        oh_all = sb("oh_all", [P, E, TILES], BF16)

        zero = sb("zero", [P, 512], BF16)
        spare = sb("spare", [P, 1])
        stats = sb("stats", [P, 2, TG, 6])
        mv = sb("mv", [P, 2, TG, 2])
        nrm = sb("nrm", [P, 2, 6, TG])
        xn_s = sb("xn_s", [P, 2, TG, D])
        xt_s = sb("xt_s", [P, 2, KH, GT])
        lg = sb("lg", [P, 2, 3, TG, E])
        best = sb("best", [P, 2, 2, TG])

        cin = before_xst([P, E, TILES])
        place = before_xst([P, E, TILES])
        rt = sb("rt", [P, 10, E])
        qi = sb("qi", [P, E], I32)
        vi = sb("vi", [P, 4, TILES], I32)
        item = sb("item", [P, 4])
        item_row = sb("item_row", [1, 2 * P], I32)

        st2 = sb("st2", [P, TB, 6])
        ms = sb("ms", [P, TB, 2])
        r2 = sb("r2", [P, 2, TB])
        p_b = sb("p_b", [P, TB + 1, R])
        e_b = sb("e_b", [P, TB + 1, R])
        tmp_e = before_xst([P, TB, R])
        qe = sb("qe", [P, TB, 3, 2 * R])
        macc = before_xst([P, KH, 2 * R, CB])
        acc = before_xst([P, KH, 2 * R, CB])
        sraw = sb("sraw", [2, R, CB])
        sacc = sb("sacc", [2, R, CB])
        accm = before_xst([P, KH, 2, P])
        sqb = before_xst([P, 2, KH, P])
        saccm = sb("saccm", [2, 2, P])
        sqa = before_xst([P, 2, D])
        cols = sb("cols", [P, 6, 2])
        dnb = before_xst([P, 2, P])
        beff = before_xst([P, 2, KH, P])
        aeff = before_xst([P, 2, D])
        midm = before_xst([P, 2, GT])

        w1_s = sb("w1_s", [P, RING, KH * H + 1])
        w2_s = sb("w2_s", [H + 1, RING, D])
        h_s = sb("h_s", [H + 1, RING, P])
        y_s = sb("y_s", [P, RING, D])
        xs_s = xn_s
        YG = 8
        yg = xt_s[:].rearrange("p h k n -> p (h k n)").rearrange("p (s d) -> p s d", d=D)

        ps = ctx.enter_context(nc.psum_tensor("ps", [P, 8, 512], F32))

        x_in, early_in, late_in = pair("x_in"), sem("early_in"), sem("late_in")
        dv = sem("dv")
        wa_ps, w64_ok, g1_ps, setup_ok = sem("wa_ps"), sem("w64_ok"), sem("g1_ps"), sem("setup_ok")
        var_ok, dev_ok, rstd_ok = pair("var_ok"), pair("dev_ok"), pair("rstd_ok")
        xn_ok, tr_ps, xt_ok, lg_ps = pair("xn_ok"), pair("tr_ps"), pair("xt_ok"), pair("lg_ps")
        xn_kept, xt_kept, ep_ok, oh_ok = pair("xn_kept"), pair("xt_kept"), pair("ep_ok"), pair("oh_ok")
        lg_read = pair("lg_read")
        rank_ps, item_ok, item_ps, place_ok, row_ok = (sem(n) for n in ("rank_ps", "item_ok", "item_ps", "place_ok", "row_ok"))
        scattered = sem("scattered")
        xt_back, xn_back, o_ps = pair("xt_back"), pair("xn_back"), pair("o_ps")
        v2_ok, sd2_ok, pb_ok, eb_ok, sh_ps, q_ok, e_ok = (sem(n) for n in ("v2_ok", "sd2_ok", "pb_ok", "eb_ok", "sh_ps", "q_ok", "e_ok"))
        accm_ok = sem("accm_ok")
        acc_ps, macc_ok, acc_ok, at_ps, sqa_ok, sqb_ok, cb_ps = (sem(n) for n in ("acc_ps", "macc_ok", "acc_ok", "at_ps", "sqa_ok", "sqb_ok", "cb_ps"))
        cb_ok, nsq_ps, nsq_ok, tn_ok, nb_ps, beff_ok, aeff_ok = (sem(n) for n in ("cb_ok", "nsq_ps", "nsq_ok", "tn_ok", "nb_ps", "beff_ok", "aeff_ok"))
        mid_ps, mid_ok, o_read = sem("mid_ps"), sem("mid_ok"), sem("o_read")
        xs_in, xst_ps, xst_ok = pair("xs_in"), pair("xst_ps"), pair("xst_ok")
        w_in, h_ps, h_ok, y_ps, y_ok, y_out = ([sem(f"{n}{s}") for s in range(RING)] for n in ("w_in", "h_ps", "h_ok", "y_ps", "y_ok", "y_out"))
        pad_ok = sem("pad_ok")
        yg_in = [sem(f"yg_in{s}") for s in range(YG)]
        added = [sem(f"added{s}") for s in range(YG)]
        stored = sem("stored")
        gp = sem("gp")

        tr = [ps[:, 0:2, :], ps[:, 2:4, :]]
        lgp = [ps[:, 4 + h, 0:TG * 64].rearrange("p (t c) -> p t c", t=TG) for h in range(2)]
        wa = ps[:, 6, 0:KH * R].rearrange("p (k r) -> p k r", k=KH)
        g1p = ps[:, 7, 0:2 * R].rearrange("p (k r) -> p k r", k=2)
        wsp = ps[0:2, 7, 256:512]
        rank = ps[:, 0:2, :].rearrange("p b n -> p (b n)")
        total = ps[:, 2:4, :].rearrange("p b n -> p (b n)")
        rowp = ps[0:1, 6, 256:512]
        shp = [ps[:, h, 0:TG * 96].rearrange("p (t g c) -> p t g c", t=TG, g=3) for h in range(2)]
        sp_ = ps[0:2, 0, :]
        accp = ps[:, 2:4, :]
        atp = [ps[:, 0, 0:D], ps[:, 1, 0:D]]
        cbp, nsqp = ps[:, 1, 256:258], ps[:, 1, 258:260]
        nbp = [ps[:, h, 384:512] for h in range(2)]
        midp = [ps[:, 2, :], ps[:, 3, :]]
        op = [ps[:, 4 + t // 2, (t % 2) * D:(t % 2 + 1) * D] for t in range(TB)]
        hp = [ps[0:H, 4 + s // 2, (s % 2) * P:(s % 2 + 1) * P] for s in range(RING)]
        hp = [ps[0:H, s, 0:P] for s in range(RING)]
        yp = [ps[:, 4 + s, 0:D] for s in range(RING)]

        x_v = x.rearrange("(t p) d -> p t d", p=P)
        out_v = out.rearrange("(t p) d -> p t d", p=P)
        xs_v = xs_dram.rearrange("(t p) d -> p t d", p=P)
        y_v = y_dram.rearrange("(i p) d -> i p d", p=P)

        block = ctx.enter_context(nc.Block())

        @block.sync
        def _(sync):
            for free in (*rstd_ok, *o_ps, *xst_ps, *y_ps):
                sync.sem_inc(free, CREDIT)
            sync.dma_start(e_sb[:], early).then_inc(early_in, 16)
            with sync.Fori(0, BATCHES) as b:
                for h in range(2):
                    if h is not None:
                        sync.wait_ge(rstd_ok[h], CREDIT + b)
                    sync.dma_start(x_all[:, bass.ds(b * TB + h * TG, TG), :],
                                   x_v[:, bass.ds(b * TB + h * TG, TG), :]).then_inc(x_in[h], 16)
            sync.dma_start(l_sb[:], late).then_inc(late_in, 16)
            with sync.Fori(0, BATCHES) as b:
                for h in range(2):
                    sync.wait_ge(xt_kept[h], CREDIT + BATCHES)
                    sync.wait_ge(xn_kept[h], CREDIT + BATCHES)
                    sync.wait_ge(o_ps[h], CREDIT + b)
                    sync.wait_ge(lg_ps[h], CREDIT + BATCHES)
                    sync.dma_start(xt_s[:, h], xt_all[:, b * 2 + h]).then_inc(xt_back[h], 16)
                    sync.dma_start(xn_s[:, h], xn_all[:, bass.ds(b * TB + h * TG, TG), :]).then_inc(xn_back[h], 16)
            sync.wait_ge(scattered, 16 * TILES)
            with sync.Fori(0, BATCHES) as b:
                for h in range(2):
                    sync.wait_ge(o_ps[h], CREDIT + BATCHES)
                    sync.wait_ge(xst_ps[h], CREDIT + b)
                    sync.dma_start(xs_s[:, h], xs_v[:, bass.ds(b * TB + h * TG, TG), :]).then_inc(xs_in[h], 16)
            sync.wait_ge(row_ok, 1)
            with sync.Fori(0, ITEMS // RING) as i:
                for s in range(RING):
                    expert = sync.value_load(item_row[0:1, bass.ds(i * RING + s, 1)], min_val=0, max_val=E - 1)
                    sync.wait_ge(y_ps[s], CREDIT + i)
                    sync.dma_start(w1_s[:, s], w1p[bass.ds(expert, 1)].rearrange("e p c -> p (e c)")).then_inc(w_in[s], 16)
                    sync.dma_start(w2_s[:, s], w2p[bass.ds(expert, 1)].rearrange("e p c -> p (e c)")).then_inc(w_in[s], 16)
            with sync.Fori(0, TILES // YG) as i:
                for s in range(YG):
                    sync.wait_ge(added[s], i + 1)
                    sync.dma_start(out_v[:, bass.ds(i * YG + s, 1), :], x_all[:, bass.ds(i * YG + s, 1), :]).then_inc(stored, 16)
            sync.wait_ge(stored, 16 * TILES)

        @block.gpsimd
        def _(pool):
            clear = [(h_s[H:H + 1], 1.0),
                     (zero[:], 0.0), (p_b[:, 0], 0.0), (e_b[:, TB], 0.0), (qe[:, :, 0, R:], 0.0), (macc[:, :, :, 0:1], 0.0),
                     (sraw[:, :, 0:1], 0.0), (reset[:], 1.0), (reset2[:], 1.0),
                     (reset[:, :, 0:1], 0.0), (reset2[:, :, 0:1], 0.0)]
            for i, (what, value) in enumerate(clear):
                nc.gpsimd.memset(what, value).then_inc(pad_ok, 1)
                pool.wait_ge(pad_ok, i + 1)
            with pool.Fori(0, BATCHES) as b:
                for h in range(2):
                    pool.wait_ge(xn_ok[h], CREDIT + b + 1)
                    nc.gpsimd.tensor_copy(xn_all[:, bass.ds(b * TB + h * TG, TG), :], xn_s[:, h]).then_inc(xn_kept[h], 1)
                    pool.wait_ge(xt_ok[h], CREDIT + b + 1)
                    nc.gpsimd.tensor_copy(xt_all[:, b * 2 + h], xt_s[:, h]).then_inc(xt_kept[h], 1)
            pool.wait_ge(place_ok, 1)
            pool.wait_ge(xn_kept[0], CREDIT + BATCHES)
            pool.wait_ge(xn_kept[1], CREDIT + BATCHES)
            for t in range(TILES):
                pool.indirect_dma_start(xs_dram, bass.IndirectOffsetOnAxis(vi[:, 1, t:t + 1], axis=0),
                                        xn_all[:, t, :], None).then_inc(scattered, 16)
            pool.wait_ge(o_ps[0], CREDIT + BATCHES)
            pool.wait_ge(o_ps[1], CREDIT + BATCHES)
            nc.gpsimd.memset(xst[:, :, N:], 0.0).then_inc(pad_ok, 1)
            for s in range(RING):
                pool.wait_ge(y_out[s], CREDIT + 16 * (ITEMS // RING))
            for t in range(TILES):
                if t >= YG:
                    pool.wait_ge(added[t % YG], t // YG)
                pool.indirect_dma_start(yg[:, t % YG, :], None, y_dram,
                                        bass.IndirectOffsetOnAxis(vi[:, 3, t:t + 1], axis=0)).then_inc(yg_in[t % YG], 16)

        @block.scalar
        def _(act):
            for free in (*xn_kept, *tr_ps, *xt_kept, *lg_ps, sh_ps, acc_ok, cb_ok):
                act.sem_inc(free, CREDIT)
            with act.Fori(0, BATCHES) as b:
                for h in range(2):
                    act.wait_ge(var_ok[h], b + 1)
                    nc.scalar.activation(nrm[:, h, 1], nrm[:, h, 0], ACT.Sqrt).then_inc(dev_ok[h], 1)
                    act.wait_ge(rstd_ok[h], CREDIT + b + 1)
                    act.wait_ge(xn_kept[h], CREDIT + b)
                    act.wait_ge(tr_ps[h], CREDIT + b)
                    for t in range(TG):
                        last = nc.scalar.activation(xn_s[:, h, t], x_all[:, b * TB + h * TG + t], ACT.Identity,
                                                    bias=nrm[:, h, 3, t:t + 1], scale=nrm[:, h, 2, t:t + 1])
                    last.then_inc(xn_ok[h], 1)
                for h in range(2):
                    act.wait_ge(tr_ps[h], CREDIT + b + 1)
                    act.wait_ge(xt_kept[h], CREDIT + b)
                    act.wait_ge(lg_ps[h], CREDIT + b)
                    nc.scalar.activation(xt_s[:, h], tr[h], ACT.Copy).then_inc(xt_ok[h], 1)
                for h in range(2):
                    act.wait_ge(lg_read[h], b + 1)
                    nc.scalar.activation(ep_all[:, bass.ds(b * TB + h * TG, TG), :], lgp[h][:, :, E:], ACT.Copy).then_inc(ep_ok[h], 1)
            act.wait_ge(pad_ok, CLEARED)
            with act.Fori(0, BATCHES) as b:
                act.wait_ge(sh_ps, CREDIT + 2 * b)
                nc.scalar.activation(p_b[:, 1:], ep_all[:, bass.ds(b * TB, TB), R:], ACT.Copy).then_inc(pb_ok, 1)
                act.wait_ge(v2_ok, b + 1)
                nc.scalar.activation(ms[:, :, 1], ms[:, :, 1], ACT.Sqrt).then_inc(sd2_ok, 1)
                for h in range(2):
                    act.wait_ge(q_ok, 2 * b + h + 1)
                    nc.scalar.activation(qe[:, h * TG:(h + 1) * TG, 1:3, R:], shp[h][:, :, 1:3, R:], ACT.Copy).then_inc(e_ok, 1)
                act.wait_ge(acc_ps, CREDIT + b + 1)
                act.wait_ge(acc_ok, CREDIT + b)
                for k in range(KH):
                    nc.scalar.activation(macc[:, k, :, 1:], accp[:, k, 0:(CB - 1) * 2 * R].rearrange("p (c r) -> p r c", r=2 * R), ACT.Copy)
                nc.scalar.activation(sraw[:, :, 1:], sp_[:, 0:(CB - 1) * 2 * R].rearrange("p (c r) -> p r c", r=2 * R)[:, 0:R, :],
                                     ACT.Copy).then_inc(macc_ok, 1)
                act.wait_ge(acc_ok, CREDIT + b + 1)
                for k in range(KH):
                    nc.scalar.activation(accm[:, k].rearrange("p h (r c) -> p h r c", c=CG),
                                         acc[:, k, 0:R, :].rearrange("p r (h c) -> p h r c", c=CG), ACT.Copy)
                nc.scalar.activation(saccm[:].rearrange("p h (r c) -> p h r c", c=CG),
                                     sacc[:].rearrange("p r (h c) -> p h r c", c=CG), ACT.Copy).then_inc(accm_ok, 1)
                for h in range(2):
                    act.wait_ge(at_ps, 2 * b + h + 1)
                    act.wait_ge(cb_ok, CREDIT + b)
                    nc.scalar.activation(sqa[:, h], atp[h], ACT.Square, accum_out=cols[:, 0, h:h + 1]).then_inc(sqa_ok, 1)
                act.wait_ge(nsq_ok, b + 1)
                nc.scalar.activation(cols[:, 3], cols[:, 2], ACT.Sqrt, scale=LR * LR).then_inc(tn_ok, 1)
            with act.Fori(0, BATCHES) as b:
                for h in range(2):
                    act.wait_ge(xst_ps[h], CREDIT + b + 1)
                    nc.scalar.activation(xst[:, 1, bass.ds((b * 2 + h) * GT, GT)], tr[h][:, 1], ACT.Copy).then_inc(xst_ok[h], 1)

            def store(i, s):
                act.wait_ge(y_ok[s], CREDIT + i + 1)
                act.dma_start(y_v[bass.ds(i * RING + s, 1)].rearrange("i p d -> p (i d)"), y_s[:, s]).then_inc(y_out[s], 16)

            with act.Fori(0, ITEMS // RING) as i:
                for s in range(RING):
                    act.wait_ge(h_ps[s], i + 1)
                    nc.scalar.activation(h_s[0:H, s], hp[s], ACT.Relu, bias=w1_s[0:H, s, KH * H:]).then_inc(h_ok[s], 1)
                    if s:
                        store(i, s - 1)
                store(i, RING - 1)

        @block.vector
        def _(dve):
            for free in (*xn_ok, acc_ps, *y_out):
                dve.sem_inc(free, CREDIT)
            vec = nc.vector
            n = Count(0)

            def mine(instruction):
                instruction.then_inc(dv, 1)
                dve.wait_ge(dv, n())

            dve.wait_ge(early_in, 16)
            dve.wait_ge(wa_ps, 1)
            for k in range(KH):
                vec.tensor_scalar(w64[:, k, E:E + R], wa[:, k], gb[:, k, 0:1], None, ALU.mult)
                last = vec.tensor_scalar(bwa[:, k], wa[:, k], gb[:, k, 1:2], None, ALU.mult)
            last.then_inc(w64_ok, 1)

            STEPS1 = 22
            with dve.Fori(0, BATCHES) as b:
                def norm(h):
                    dve.wait_ge(x_in[h], 16 * (b + 1))
                    for t in range(TG):
                        last = vec.bn_stats(stats[:, h, t], x_all[:, b * TB + h * TG + t])
                    last.then_inc(dv, 1)
                    dve.wait_ge(dv, n())
                    vec.memset(spare[:], 0.0)
                    for t in range(TG):
                        last = vec.bn_aggr(mv[:, h, t], stats[:, h, t])
                    mine(last)
                    vec.tensor_scalar(nrm[:, h, 0], mv[:, h, :, 1], EPS, None, ALU.add).then_inc(var_ok[h], 1)
                    dve.wait_ge(dev_ok[h], b + 1)
                    mine(vec.reciprocal(nrm[:, h, 4], nrm[:, h, 1]))
                    mine(vec.tensor_tensor(nrm[:, h, 5], nrm[:, h, 4], nrm[:, h, 4], ALU.mult))
                    mine(vec.tensor_tensor(nrm[:, h, 5], nrm[:, h, 5], nrm[:, h, 0], ALU.mult))
                    mine(vec.tensor_scalar(nrm[:, h, 5], nrm[:, h, 5], -0.5, 1.5, ALU.mult, ALU.add))
                    dve.wait_ge(xn_ok[h], CREDIT + b)
                    mine(vec.tensor_tensor(nrm[:, h, 2], nrm[:, h, 4], nrm[:, h, 5], ALU.mult))
                    vec.scalar_tensor_tensor(nrm[:, h, 3], mv[:, h, :, 0], -1.0, nrm[:, h, 2], ALU.mult, ALU.mult).then_inc(rstd_ok[h], 1)

                def choose(h):
                    dve.wait_ge(lg_ps[h], CREDIT + b + 1)
                    rb = col["rb"].unsqueeze(1).broadcast_to([P, TG, E])
                    vec.tensor_tensor(lg[:, h, 0], lgp[h][:, :, 0:E], rb, ALU.add).then_inc(lg_read[h], 1)
                    dve.wait_ge(lg_read[h], b + 1)
                    mine(vec.tensor_reduce(best[:, h, 0], lg[:, h, 0], AX.X, ALU.max))
                    b0 = best[:, h, 0].unsqueeze(2).broadcast_to([P, TG, E])
                    mine(vec.tensor_tensor(lg[:, h, 1], lg[:, h, 0], b0, ALU.is_ge))
                    mine(vec.tensor_tensor(lg[:, h, 2], lg[:, h, 1], edesc.unsqueeze(1).broadcast_to([P, TG, E]), ALU.mult))
                    mine(vec.tensor_reduce(best[:, h, 1], lg[:, h, 2], AX.X, ALU.max))
                    b1 = best[:, h, 1].unsqueeze(2).broadcast_to([P, TG, E])
                    vec.tensor_tensor(oh_all[:, :, bass.ds(b * TB + h * TG, TG)].rearrange("p e t -> p t e"),
                                      lg[:, h, 2], b1, ALU.is_equal).then_inc(oh_ok[h], 1)

                n = Count(b * STEPS1)
                norm(0)
                norm(1)
                choose(0)
                choose(1)
                assert n.k == STEPS1, n.k
            n = Count(STEPS1 * BATCHES)

            dve.wait_ge(late_in, 16)
            for k in range(KH):
                vec.tensor_scalar(wpgt[:, k], wpt[:, k], gb[:, k, 0:1], None, ALU.mult)
                vec.tensor_scalar(gbn[:, k, 0:1], gb[:, k, 0:1], -1.0, None, ALU.mult)
                vec.tensor_copy(gbn[:, k, 1:2], gb[:, k, 1:2])
            vec.tensor_scalar(at2[:], col["atrep"], SCALING, None, ALU.mult)
            vec.tensor_copy(ones_bf[:], ones)
            vec.tensor_copy(ntri_bf[:], col["ntri"]).then_inc(setup_ok, 1)
            dve.wait_ge(g1_ps, 1)
            vec.tensor_copy(g1b1[:], g1p)
            vec.tensor_copy(ws[:], wsp).then_inc(setup_ok, 1)

            flat = lambda t: t.rearrange("p e t -> p (e t)")
            num, tiles, cn, ct, off, dist, pack, cmp, sel = (rt[:, i] for i in range(9))
            dve.wait_ge(rank_ps, 1)
            dve.wait_ge(pad_ok, CLEARED)
            mine(vec.tensor_tensor_scan(flat(cin[:]), flat(reset[:]), total, 0.0, ALU.mult, ALU.add))
            vec.tensor_tensor(flat(place[:]), rank, flat(cin[:]), ALU.add).then_inc(dv, 1)
            num = cin[:, :, TILES - 1]
            vec.tensor_scalar(qi[:], num, float(P - 1), None, ALU.add).then_inc(dv, 1)
            dve.wait_ge(dv, n(2))
            mine(vec.tensor_scalar(qi[:], qi[:], 7, 7, ALU.arith_shift_right, ALU.logical_shift_left))
            mine(vec.tensor_copy(tiles, qi[:]))
            vec.tensor_tensor_scan(cn, reset[:, 0:1, 1:2].rearrange("p a b -> p (a b)").broadcast_to([P, E]), num, 0.0, ALU.mult, ALU.add).then_inc(dv, 1)
            vec.tensor_tensor_scan(ct, reset[:, 0:1, 1:2].rearrange("p a b -> p (a b)").broadcast_to([P, E]), tiles, 0.0, ALU.mult, ALU.add).then_inc(dv, 1)
            dve.wait_ge(dv, n(2))
            mine(vec.tensor_tensor(off, cn, num, ALU.subtract))
            mine(vec.tensor_tensor(dist, ct, tiles, ALU.subtract))
            mine(vec.tensor_tensor(dist, dist, off, ALU.subtract))
            mine(vec.scalar_tensor_tensor(pack, dist, float(PK), off, ALU.mult, ALU.add))
            mine(vec.tensor_tensor(place[:], place[:], pack.unsqueeze(2).broadcast_to([P, E, TILES]), ALU.add))
            mine(vec.tensor_tensor(place[:], place[:], oh_all[:], ALU.mult))
            mine(vec.tensor_reduce(item_sum := cin[:, 0], place[:].rearrange("p e t -> p t e"), AX.X, ALU.add))
            mine(vec.tensor_copy(vi[:, 0], item_sum))
            vec.tensor_scalar(vi[:, 1], vi[:, 0], PK - 1, None, ALU.bitwise_and).then_inc(dv, 1)
            vec.tensor_scalar(vi[:, 2], vi[:, 0], 12, None, ALU.arith_shift_right).then_inc(dv, 1)
            dve.wait_ge(dv, n(2))
            vec.tensor_tensor(vi[:, 3], vi[:, 1], vi[:, 2], ALU.add).then_inc(place_ok, 1)
            mine(vec.tensor_scalar(cmp, ct, icol, None, ALU.is_le))
            mine(vec.tensor_reduce(item[:, 2:3], cmp, AX.X, ALU.add))
            mine(vec.tensor_scalar(item[:, 0:1], item[:, 2:3], float(E - 1), None, ALU.min))
            mine(vec.scalar_tensor_tensor(sel, eiota, item[:, 0:1], dist, ALU.is_equal, ALU.mult))
            mine(vec.tensor_reduce(item[:, 3:4], sel, AX.X, ALU.add))
            mine(vec.tensor_tensor(item[:, 2:3], icol, item[:, 3:4], ALU.subtract))
            vec.tensor_scalar(item[:, 1:2], item[:, 2:3], float(N), None, ALU.min).then_inc(item_ok, 1)
            dve.wait_ge(item_ps, 1)
            vec.tensor_copy(item_row[:], rowp).then_inc(row_ok, 1)

            first, PER2 = n.k + n.at, 16
            with dve.Fori(0, BATCHES) as b:
                n = Count(first + b * PER2)
                dve.wait_ge(acc_ps, CREDIT + b)
                for t in range(TB):
                    last = vec.bn_stats(st2[:, t], xn_all[:, b * TB + t])
                    if t == 0:
                        dve.wait_ge(xn_kept[0], CREDIT + BATCHES)
                        dve.wait_ge(xn_kept[1], CREDIT + BATCHES)
                last.then_inc(dv, 1)
                dve.wait_ge(dv, n())
                vec.memset(spare[:], 0.0)
                for t in range(TB):
                    last = vec.bn_aggr(ms[:, t], st2[:, t])
                mine(last)
                vec.tensor_scalar(ms[:, :, 1], ms[:, :, 1], EPS, None, ALU.add).then_inc(v2_ok, 1)
                dve.wait_ge(sd2_ok, b + 1)
                mine(vec.reciprocal(r2[:, 0], ms[:, :, 1]))
                mine(vec.scalar_tensor_tensor(r2[:, 1], ms[:, :, 0], -1.0, r2[:, 0], ALU.mult, ALU.mult))
                wide = lambda v: v.unsqueeze(2).broadcast_to([P, TB, R])
                same = lambda v: v.unsqueeze(1).broadcast_to([P, TB, R])
                vec.tensor_tensor(tmp_e[:], ep_all[:, bass.ds(b * TB, TB), 0:R], wide(r2[:, 0]), ALU.mult).then_inc(dv, 1)
                dve.wait_ge(sh_ps, CREDIT + 2 * b)
                vec.tensor_tensor(e_b[:, 0:TB], wide(r2[:, 1]), same(g1b1[:, 0]), ALU.mult).then_inc(dv, 1)
                dve.wait_ge(dv, n(2))
                mine(vec.tensor_tensor(tmp_e[:], tmp_e[:], e_b[:, 0:TB], ALU.add))
                vec.tensor_tensor(e_b[:, 0:TB], tmp_e[:], same(g1b1[:, 1]), ALU.add).then_inc(eb_ok, 1)
                for h in range(2):
                    dve.wait_ge(sh_ps, CREDIT + 2 * b + h + 1)
                    for g in range(3):
                        last = vec.tensor_tensor(qe[:, h * TG:(h + 1) * TG, g, 0:R], shp[h][:, :, g, 0:R],
                                                 r2[:, 0, h * TG:(h + 1) * TG].unsqueeze(2).broadcast_to([P, TG, R]), ALU.mult)
                    last.then_inc(q_ok, 1)
                dve.wait_ge(macc_ok, b + 1)
                mine(vec.tensor_tensor_scan(acc[:].rearrange("p k r c -> p (k r c)"), reset2[:].rearrange("p a c -> p (a c)"),
                                            macc[:].rearrange("p k r c -> p (k r c)"), 0.0, ALU.mult, ALU.add))
                vec.tensor_tensor_scan(sacc[:].rearrange("p r c -> p (r c)"), reset2[0:2, 0:R].rearrange("p a c -> p (a c)"),
                                       sraw[:].rearrange("p r c -> p (r c)"), 0.0, ALU.mult, ALU.add).then_inc(acc_ok, 1)
                for h in range(2):
                    for k in range(KH):
                        v = acc[:, k, R:, h * CG:(h + 1) * CG]
                        last = vec.tensor_tensor(sqb[:, h, k].rearrange("p (r c) -> p r c", c=CG), v, v, ALU.mult)
                last.then_inc(sqb_ok, 1)
                dve.wait_ge(cb_ps, b + 1)
                dve.wait_ge(sqa_ok, 2 * b + 2)
                vec.tensor_tensor(cols[:, 1], cbp, cols[:, 0], ALU.add).then_inc(cb_ok, 1)
                dve.wait_ge(nsq_ps, b + 1)
                vec.tensor_scalar(cols[:, 2], nsqp, 1e-30, None, ALU.max).then_inc(nsq_ok, 1)
                dve.wait_ge(tn_ok, b + 1)
                mine(vec.tensor_scalar(cols[:, 4], cols[:, 3], 1e-6, None, ALU.add))
                mine(vec.reciprocal(cols[:, 5], cols[:, 4]))
                mine(vec.tensor_scalar(cols[:, 4], cols[:, 5], 1.0, -LR, ALU.min, ALU.mult))
                mine(vec.tensor_scalar(cols[:, 5], cols[:, 4], SCALING, None, ALU.mult))
                for h in range(2):
                    vec.tensor_scalar(dnb[:, h], ident, cols[:, 4, h:h + 1], None, ALU.mult)
                for h in range(2):
                    last = vec.scalar_tensor_tensor(aeff[:, h], atp[h], cols[:, 5, h:h + 1], at2[:], ALU.mult, ALU.add)
                last.then_inc(aeff_ok, 1)
                for h in range(2):
                    dve.wait_ge(nb_ps, 2 * b + h + 1)
                    for k in range(KH):
                        vec.tensor_tensor(beff[:, h, k].rearrange("p (r c) -> p r c", c=CG), acc[:, k, R:, h * CG:(h + 1) * CG],
                                          nbp[h].rearrange("p (r c) -> p r c", c=CG), ALU.mult).then_inc(dv, 1)
                    dve.wait_ge(dv, n(2))
                    vec.tensor_tensor(beff[:, h], beff[:, h], btrep, ALU.add).then_inc(beff_ok, 1)
                for h in range(2):
                    dve.wait_ge(mid_ps, 2 * b + h + 1)
                    vec.tensor_tensor(midm[:, h], midp[h], diag, ALU.mult).then_inc(mid_ok, 1)
                for h in range(2):
                    dve.wait_ge(o_ps[h], CREDIT + b + 1)
                    for q in range(TG // 2):
                        t = h * TG + 2 * q
                        xo = x_all[:, bass.ds(b * TB + t, 2), :]
                        last = vec.tensor_tensor(xo, ps[:, 4 + t // 2, :].rearrange("p (t d) -> p t d", t=2), xo, ALU.add)
                    last.then_inc(o_read, 1)
                per = n.k
                assert per == PER2, per

            with dve.Fori(0, BATCHES) as b:
                for h in range(2):
                    dve.wait_ge(xst_ps[h], CREDIT + b + 1)
                    vec.tensor_copy(xst[:, 0, bass.ds((b * 2 + h) * GT, GT)], tr[h][:, 0]).then_inc(xst_ok[h], 1)
            with dve.Fori(0, ITEMS // RING) as i:
                for s in range(RING):
                    dve.wait_ge(y_ps[s], CREDIT + i + 1)
                    dve.wait_ge(y_out[s], CREDIT + 16 * i)
                    vec.tensor_scalar(y_s[:, s], yp[s], 0.0, None, ALU.max).then_inc(y_ok[s], 1)
            with dve.Fori(0, TILES // YG) as i:
                for s in range(YG):
                    dve.wait_ge(yg_in[s], 16 * (i + 1))
                    xo = x_all[:, i * YG + s]
                    vec.tensor_tensor(xo, xo, yg[:, s], ALU.add).then_inc(added[s], 1)

        @block.tensor
        def _(pe):
            for free in (*xt_ok, *oh_ok, *ep_ok, beff_ok, o_read, mid_ok, *xst_ok, *h_ok, *y_ok):
                pe.sem_inc(free, CREDIT)
            mm = nc.tensor.matmul
            pe.wait_ge(early_in, 16)
            for m in range(KH):
                for k in range(KH):
                    last = mm(wa[:, m], wp[:, k, m * P:(m + 1) * P], a_w[:, k], start=(k == 0), stop=(k == KH - 1))
            last.then_inc(wa_ps, 1)

            def transpose_group(h, source, done):
                for t in range(TG):
                    for k in range(KH):
                        last = nc.tensor.transpose(tr[h][:, k, t * P:(t + 1) * P], source[:, h, t, k * P:(k + 1) * P], ident)
                last.then_inc(done, 1)

            with pe.Fori(0, BATCHES) as b:
                for h in range(2):
                    pe.wait_ge(xn_ok[h], CREDIT + b + 1)
                    pe.wait_ge(xt_ok[h], CREDIT + b)
                    transpose_group(h, xn_s, tr_ps[h])
                pe.wait_ge(w64_ok, 1)
                for h in range(2):
                    pe.wait_ge(xt_ok[h], CREDIT + b + 1)
                    pe.wait_ge(oh_ok[h], CREDIT + b)
                    pe.wait_ge(ep_ok[h], CREDIT + b)
                    for t in range(TG):
                        for k in range(KH):
                            last = mm(lgp[h][:, t], xt_s[:, h, k, t * P:(t + 1) * P], w64[:, k], start=(k == 0), stop=(k == KH - 1))
                    last.then_inc(lg_ps[h], 1)
            pe.wait_ge(setup_ok, 1)
            for k in range(KH):
                mm(g1p[:, 0], ones, w64[:, k, E:E + R], start=(k == 0), stop=(k == KH - 1))
            for k in range(KH):
                mm(g1p[:, 1], ones, bwa[:, k], start=(k == 0), stop=(k == KH - 1))
            for k in range(KH):
                last = mm(wsp, gbn[:, k], wpt[:, k], start=(k == 0), stop=(k == KH - 1))
            last.then_inc(g1_ps, 1)
            for h in range(2):
                pe.wait_ge(oh_ok[h], CREDIT + BATCHES)
                pe.wait_ge(xt_ok[h], CREDIT + BATCHES)
            oh = oh_all[:].rearrange("p e t -> p (e t)")
            for c in range(2):
                mm(total[:, c * 512:(c + 1) * 512], ones_bf[:], oh[:, c * 512:(c + 1) * 512], start=True, stop=True)
            for c in range(2):
                last = mm(rank[:, c * 512:(c + 1) * 512], ntri_bf[:], oh[:, c * 512:(c + 1) * 512], start=True, stop=True)
            last.then_inc(rank_ps, 1)
            pe.wait_ge(item_ok, 1)
            for c in range(2):
                last = nc.tensor.transpose(rowp[:, c * P:(c + 1) * P], item[:, c:c + 1], ident)
            last.then_inc(item_ps, 1)

            pe.wait_ge(setup_ok, 2)
            pe.wait_ge(pad_ok, CLEARED)
            pe.wait_ge(row_ok, 1)
            with pe.Fori(0, BATCHES) as b:
                pe.wait_ge(pb_ok, b + 1)
                pe.wait_ge(eb_ok, b + 1)
                pe.wait_ge(beff_ok, CREDIT + 2 * b)
                for h in range(2):
                    t0, t1 = h * TG, (h + 1) * TG
                    mm(shp[h][:, :, 0, 0:R], shift[0], p_b[:, t0:t1], start=True, stop=False)
                    mm(shp[h][:, :, 1, 0:R], shift[1], p_b[:, t0 + 1:t1 + 1], start=False, stop=False)
                    mm(shp[h][:, :, 2, 0:R], shift[2], p_b[:, t0 + 1:t1 + 1], start=False, stop=False)
                    mm(shp[h][:, :, 1, R:], shift[3], e_b[:, t0:t1], start=False, stop=False)
                    mm(shp[h][:, :, 2, R:], shift[4], e_b[:, t0:t1], start=False, stop=False)
                    mm(shp[h][:, :, 2, R:], shift[5], e_b[:, t0 + 1:t1 + 1], start=False, stop=True).then_inc(sh_ps, 1)

                def base(h):
                    pe.wait_ge(xt_back[h], 16 * (b + 1))
                    pe.wait_ge(o_read, CREDIT + 2 * b)
                    for t in range(TG):
                        for k in range(KH):
                            mm(op[h * TG + t], xt_s[:, h, k, t * P:(t + 1) * P], wbt[:, k], start=(k == 0 and t % 2 == 0), stop=False)

                base(0)
                pe.wait_ge(q_ok, 2 * b + 2)
                pe.wait_ge(e_ok, 2 * b + 2)
                pe.wait_ge(mid_ok, CREDIT + 2 * b)
                for k in range(KH):
                    mm(accp[:, k], zero[:, 0:P], zero[:, 0:512], start=True, stop=False)
                mm(sp_, zero[:, 0:2], zero[:, 0:512], start=True, stop=False)
                for t in range(TB):
                    if t % TG == 0:
                        pe.wait_ge(xn_back[t // TG], 16 * (b + 1))
                    g = 1 if t == 0 else 0
                    rhs = qe[:, t, g:]
                    cols_ = slice((2 * t - 1 + g) * 2 * R, (2 * t + 2) * 2 * R)
                    for k in range(KH):
                        mm(accp[:, k, cols_], xn_s[:, t // TG, t % TG, k * P:(k + 1) * P], rhs, start=False, stop=(t == TB - 1))
                    last = mm(sp_[:, cols_], ms[:, t], rhs, start=False, stop=(t == TB - 1))
                last.then_inc(acc_ps, 1)
                base(1)
                pe.wait_ge(accm_ok, b + 1)
                for h in range(2):
                    for k in range(KH):
                        mm(atp[h], accm[:, k, h], wpgt[:, k], start=(k == 0), stop=False)
                    mm(atp[h], saccm[:, h], ws[:], start=False, stop=True).then_inc(at_ps, 1)
                pe.wait_ge(sqb_ok, b + 1)
                pe.wait_ge(sqa_ok, 2 * b + 2)
                for h in range(2):
                    for k in range(KH):
                        last = mm(cbp[:, h:h + 1], sqb[:, h, k], ones[:, 0:1], start=(k == 0), stop=(k == KH - 1))
                last.then_inc(cb_ps, 1)
                pe.wait_ge(cb_ok, CREDIT + b + 1)
                mm(nsqp, blk, cols[:, 1], start=True, stop=True).then_inc(nsq_ps, 1)
                pe.wait_ge(aeff_ok, b + 1)
                for h in range(2):
                    mm(nbp[h], ones, dnb[:, h], start=True, stop=True).then_inc(nb_ps, 1)
                for h in range(2):
                    pe.wait_ge(beff_ok, CREDIT + 2 * b + h + 1)
                    for k in range(KH):
                        last = mm(midp[h], beff[:, h, k], xt_s[:, h, k], start=(k == 0), stop=(k == KH - 1))
                    last.then_inc(mid_ps, 1)
                pe.wait_ge(aeff_ok, b + 1)
                for h in range(2):
                    pe.wait_ge(mid_ok, CREDIT + 2 * b + h + 1)
                    for t in range(TG):
                        last = mm(op[h * TG + t], midm[:, h, t * P:(t + 1) * P], aeff[:, h], start=False, stop=(t % 2 == 1))
                    last.then_inc(o_ps[h], 1)

            pe.wait_ge(mid_ok, CREDIT + 2 * BATCHES)
            pe.wait_ge(aeff_ok, BATCHES)
            with pe.Fori(0, BATCHES) as b:
                for h in range(2):
                    pe.wait_ge(xs_in[h], 16 * (b + 1))
                    pe.wait_ge(xst_ok[h], CREDIT + 2 * b)
                    transpose_group(h, xs_s, xst_ps[h])
            for h in range(2):
                pe.wait_ge(xst_ok[h], CREDIT + 2 * BATCHES)
            pe.wait_ge(o_read, CREDIT + 2 * BATCHES)
            pe.wait_ge(pad_ok, CLEARED + 1)
            with pe.Fori(0, ITEMS // RING) as i:
                def first_layer(s):
                    first_token = pe.value_load(item_row[0:1, bass.ds(P + i * RING + s, 1)], min_val=0, max_val=N)
                    pe.wait_ge(w_in[s], 32 * (i + 1))
                    pe.wait_ge(h_ok[s], CREDIT + i)
                    for k in range(KH):
                        last = mm(hp[s], w1_s[:, s, k * H:(k + 1) * H], xst[:, k, bass.ds(first_token, P)], start=(k == 0), stop=(k == KH - 1))
                    last.then_inc(h_ps[s], 1)

                def second_layer(s):
                    pe.wait_ge(h_ok[s], CREDIT + i + 1)
                    pe.wait_ge(y_ok[s], CREDIT + i)
                    mm(yp[s], h_s[:, s], w2_s[:, s], start=True, stop=True).then_inc(y_ps[s], 1)

                first_layer(0)
                for s in range(1, RING):
                    first_layer(s)
                    second_layer(s - 1)
                second_layer(RING - 1)


def kernel(L0_attn_x, L0_attn_Wb, L0_attn_init_A, L0_attn_init_B, L0_attn_ln_gamma, L0_attn_ln_beta, L0_attn_Wp,
           L0_ffn_router_w, L0_ffn_router_b, L0_ffn_weights1, L0_ffn_bias1, L0_ffn_weights2, L0_ffn_bias2):
    import numpy as np
    import concourse.bacc as bacc
    from concourse.bass_utils import run_bass_kernel_spmd

    f = lambda a: np.ascontiguousarray(np.asarray(a))
    halves = lambda a: f(a).reshape(KH, P, -1).transpose(1, 0, 2).reshape(P, -1)
    eye = np.eye(P, dtype=np.float32)
    k, m = np.arange(P)[:, None], np.arange(P)[None, :]
    shifts = [(k == P - 1) & (m == 0), (k == m - 1) & (m <= CHUNK), (k == m - 1) & (m > CHUNK),
              (k == m + 1) & (m < CHUNK), (k == m + 1) & (m >= CHUNK), (k == 0) & (m == P - 1)]
    router, b_t = f(L0_ffn_router_w).T, f(L0_attn_init_B).T
    parts = {
        "ident": eye,
        "w64": halves(np.concatenate([router, np.zeros((D, R), np.float32), b_t], 1)),
        "rb": np.tile(f(L0_ffn_router_b), (P, 1)),
        "edesc": np.tile(E - np.arange(E), (P, 1)),
        "wp": halves(L0_attn_Wp),
        "a": halves(L0_attn_init_A),
        "gb": halves(np.stack([f(L0_attn_ln_gamma), f(L0_attn_ln_beta)], 1)),
        "eiota": np.tile(np.arange(E), (P, 1)),
        "icol": P * np.arange(P)[:, None],
        "ones": np.ones((P, P)),
        "ntri": -1.0 * (k >= m),
        "sh": np.concatenate(shifts, 1),
        "blk": k % CG == m % CG,
        "diag": k % CG == np.arange(GT)[None, :] // CHUNK,
        "wpt": halves(f(L0_attn_Wp).T),
        "wbt": halves(f(L0_attn_Wb).T),
        "atrep": np.repeat(f(L0_attn_init_A).T, CG, 0),
        "btrep": halves(np.repeat(b_t, CG, 1)),
    }
    pack = lambda names: np.concatenate([parts[n].astype(np.float32) for n, _ in names], 1)
    w1 = f(L0_ffn_weights1).reshape(E, KH, P, H).transpose(0, 2, 1, 3).reshape(E, P, KH * H)
    b1 = np.concatenate([f(L0_ffn_bias1), f(L0_ffn_bias1)], 1)[:, :, None]
    w1p = np.concatenate([w1, b1], 2)
    w2p = np.concatenate([f(L0_ffn_weights2), f(L0_ffn_bias2)[:, None, :]], 1)
    arrays = {"x": f(L0_attn_x).reshape(N, D), "early": pack(EARLY), "late": pack(LATE), "w1p": w1p, "w2p": w2p}
    nc = bacc.Bacc("TRN2", target_bir_lowering=False, num_devices=1)
    args = [nc.dram_tensor(n, list(a.shape), F32, kind="ExternalInput").ap() for n, a in arrays.items()]
    out = nc.dram_tensor("out", [N, D], F32, kind="ExternalOutput").ap()
    build(nc, *args, out)
    got = run_bass_kernel_spmd(nc, [{n: np.ascontiguousarray(a) for n, a in arrays.items()}], core_ids=[0])
    return got.results[0]["out"].reshape(L0_attn_x.shape)
```

```python
from contextlib import ExitStack

import concourse.bass as bass
from concourse import mybir
from concourse.alu_op_type import AluOpType as ALU

F32 = mybir.dt.float32
BF16 = mybir.dt.bfloat16
I32 = mybir.dt.int32
ACT = mybir.ActivationFunctionType
AX = mybir.AxisListType

P = 128
D = 256
KH = D // P
N = 4096
TILES = N // P
BATCHES = 4
TB = TILES // BATCHES
TG = TB // 2
GT = TG * P
R = 16
CHUNK = 64
CB = TB * P // CHUNK
CG = CB // 2
E = 32
H = 64
ITEMS = 64
CREDIT = 1
CLEARED = 12
RING = 8
MADE = 6
BANKS = 4
QUEUE = 8
LR = 0.01 * 2.0
SCALING = 2.0
EPS = 1e-5
PK = 1 << 12

EARLY = [("ident", P), ("w64", KH * 64), ("rb", E), ("edesc", E), ("wp", KH * D), ("a", KH * R), ("gb", KH * 2)]
LATE = [("eiota", E), ("icol", 1), ("ones", P), ("ntri", P), ("sh", 6 * P), ("blk", P), ("diag", GT),
        ("wpt", KH * D), ("wbt", KH * D), ("atrep", D), ("btrep", KH * P)]


class Count:

    def __init__(self, at):
        self.at, self.k = at, 0

    def __call__(self, k=1):
        self.k += k
        return self.at + self.k


def build(nc, x, early, late, wx, out):
    ctx = ExitStack()
    with ctx:
        def sb(name, shape, dt=F32):
            return ctx.enter_context(nc.sbuf_tensor(name, shape, dt))

        def sem(name):
            return ctx.enter_context(nc.semaphore(name))

        def pair(name):
            return [sem(f"{name}{h}") for h in range(2)]

        xs_dram = nc.dram_tensor("xs_dram", [N, D], F32, kind="Internal").ap()
        y_dram = nc.dram_tensor("y_dram", [ITEMS * P, D], F32, kind="Internal").ap()

        e_sb = sb("e_sb", [P, sum(w for _, w in EARLY)])
        l_sb = sb("l_sb", [P, sum(w for _, w in LATE)])
        col = {}
        for t, names in ((e_sb, EARLY), (l_sb, LATE)):
            at = 0
            for n, w in names:
                col[n] = t[:, at:at + w]
                at += w
        ident, edesc, eiota, icol, ones, blk, diag = (col[k] for k in ("ident", "edesc", "eiota", "icol", "ones", "blk", "diag"))
        w64 = col["w64"].rearrange("p (k c) -> p k c", k=KH)
        wp = col["wp"].rearrange("p (k d) -> p k d", k=KH)
        a_w = col["a"].rearrange("p (k r) -> p k r", k=KH)
        gb = col["gb"].rearrange("p (k c) -> p k c", k=KH)
        wpt = col["wpt"].rearrange("p (k h) -> p k h", k=KH)
        wbt = col["wbt"].rearrange("p (k h) -> p k h", k=KH)
        btrep = col["btrep"].rearrange("p (k c) -> p k c", k=KH)
        shift = [col["sh"][:, i * P:(i + 1) * P] for i in range(6)]

        wpgt = sb("wpgt", [P, KH, D])
        gbn = sb("gbn", [P, KH, 2])
        ws = sb("ws", [2, D])
        bwa = sb("bwa", [P, KH, R])
        g1b1 = sb("g1b1", [P, 2, R])
        at2 = sb("at2", [P, D])
        ones_bf = sb("ones_bf", [P, P], BF16)
        ntri_bf = sb("ntri_bf", [P, P], BF16)
        reset2 = sb("reset2", [P, KH * 2 * R, CB])

        x_all = sb("x_all", [P, TILES, D])
        xn_all = sb("xn_all", [P, TILES, D])
        xt_all = sb("xt_all", [P, TILES // TG, KH, GT])
        xst = sb("xst", [P, KH, N + P])
        shared = xst[:].rearrange("p k n -> p (k n)")
        used = [0]

        def before_xst(shape):
            size = 1
            for w in shape[1:]:
                size *= w
            view = shared[0:shape[0], used[0]:used[0] + size]
            used[0] += size
            assert used[0] <= KH * (N + P)
            names = "abcd"[:len(shape) - 1]
            return view.rearrange(f"p ({' '.join(names)}) -> p {' '.join(names)}", **dict(zip(names, shape[1:])))

        e_raw = before_xst([P, TILES, R])
        e_all = sb("e_all", [P, BATCHES, TB + 1, R])
        p_all = sb("p_all", [P, BATCHES, TB + 1, R])
        nr = sb("nr", [P, 2, TILES])
        sums = sb("sums", [P, 2, TILES])
        ms = sb("ms", [P, TILES, 2])
        r2 = sb("r2", [P, 2, TILES])

        zero = sb("zero", [P, 512], BF16)
        spare = sb("spare", [P, 1])
        stats = sb("stats", [P, TB, 6])
        mv = sb("mv", [P, TB, 2])
        nrm = sb("nrm", [P, 4, TB])
        xn_s = sb("xn_s", [P, 2, TG, D])
        xt_s = sb("xt_s", [P, 2, KH, GT])
        lg = before_xst([P, 2, 3, TG, E])
        oh_all = sb("oh_all", [P, E, TILES], BF16)
        best = sb("best", [P, 2, 2, TG])

        cin = before_xst([P, E, TILES])
        place = before_xst([P, E, TILES])
        reset = before_xst([P, E, TILES])
        rt = before_xst([P, 10, E])
        qi = sb("qi", [P, E], I32)
        vi = sb("vi", [P, 4, TILES], I32)
        item = sb("item", [P, 4])
        item_row = sb("item_row", [1, 2 * P], I32)

        ms_b = sb("ms_b", [P, TB, 2])
        tmp2 = before_xst([P, 3, TILES])
        tmp_e = lg.rearrange("p a b t e -> p (a b t e)")[:, 0:TILES * R].rearrange("p (t r) -> p t r", r=R)
        qe = sb("qe", [P, TB, 3, 2 * R])
        macc = sb("macc", [P, KH, 2 * R, CB])
        acc = cin.rearrange("p (k a) (b c) -> p k (a b) c", k=KH, c=CB)
        beff = place[:, 0:E // 2, :].rearrange("p (h k a) t -> p h k (a t)", h=2, k=KH)
        aeff = place[:, E // 2:, :].rearrange("p (h a) t -> p h (a t)", h=2)
        sraw = sb("sraw", [2, R, CB])
        sacc = sb("sacc", [2, R, CB])
        accm = before_xst([P, KH, 2, P])
        sqb = before_xst([P, 2, KH, P])
        saccm = sb("saccm", [2, 2, P])
        sqa = before_xst([P, 2, D])
        cols = sb("cols", [P, 6, 2])
        dnb = before_xst([P, 2, P])
        midm = before_xst([P, 2, GT])
        junk = midm.rearrange("p a (b d) -> p (a b) d", d=D)

        WX = KH * H + 1 + D
        w_s = sb("w_s", [P, RING, WX])
        h_s = sb("h_s", [H + 1, RING, P])
        y_s = xn_all[:, 0:RING, :]
        xs_s = xn_s

        ps = ctx.enter_context(nc.psum_tensor("ps", [P, 8, 512], F32))

        x_in, early_in, late_in = sem("x_in"), sem("early_in"), sem("late_in")
        dv = sem("dv")
        pad_ok, wa_ps, w64_ok, made_ok, g1_ps, g1_ok = (sem(n) for n in ("pad_ok", "wa_ps", "w64_ok", "made_ok", "g1_ps", "g1_ok"))
        var_ok, dev_ok, nr_ok = sem("var_ok"), sem("dev_ok"), sem("nr_ok")
        xn_ok, tr_ps, xt_ok, lg_ps, lg_read = pair("xn_ok"), pair("tr_ps"), pair("xt_ok"), pair("lg_ps"), pair("lg_read")
        xn_kept, xt_kept, ep_ok, oh_ok = pair("xn_kept"), pair("xt_kept"), pair("ep_ok"), pair("oh_ok")
        rank_ps, item_ok, item_ps, place_ok, row_ok = (sem(n) for n in ("rank_ps", "item_ok", "item_ps", "place_ok", "row_ok"))
        scattered = sem("scattered")
        sq_ok, v2_ok, sd2_ok, eb_ok = sem("sq_ok"), sem("v2_ok"), sem("sd2_ok"), sem("eb_ok")
        xt_back, xn_back, o_ps = pair("xt_back"), pair("xn_back"), pair("o_ps")
        sh_ps, q_ok, e_ok, acc_ps, macc_ok, acc_ok, accm_ok = (sem(n) for n in ("sh_ps", "q_ok", "e_ok", "acc_ps", "macc_ok", "acc_ok", "accm_ok"))
        at_ps, sqa_ok, sqb_ok, cb_ps, cb_ok, nsq_ps, nsq_ok = (sem(n) for n in ("at_ps", "sqa_ok", "sqb_ok", "cb_ps", "cb_ok", "nsq_ps", "nsq_ok"))
        tn_ok, nb_ps, beff_ok, aeff_ok, mid_ps, mid_ok = (sem(n) for n in ("tn_ok", "nb_ps", "beff_ok", "aeff_ok", "mid_ps", "mid_ok"))
        o_read = pair("o_read")
        xs_in, xst_ps, xst_ok = pair("xs_in"), pair("xst_ps"), pair("xst_ok")
        w_in, h_ps, h_ok, y_ps, y_ok = ([sem(f"{n}{s}") for s in range(RING)] for n in ("w_in", "h_ps", "h_ok", "y_ps", "y_ok"))
        y_out = pair("y_out")
        added = [sem(f"added{s}") for s in range(QUEUE)]
        stored = sem("stored")

        tr = [ps[:, 0:2, :], ps[:, 2:4, :]]
        lgp = [ps[:, 4 + h, 0:TG * 64].rearrange("p (t c) -> p t c", t=TG) for h in range(2)]
        wa = ps[:, 6, 0:KH * R].rearrange("p (k r) -> p k r", k=KH)
        g1p = ps[:, 7, 0:2 * R].rearrange("p (k r) -> p k r", k=2)
        wsp = ps[0:2, 7, 256:512]
        rank = ps[:, 0:2, :].rearrange("p b n -> p (b n)")
        total = ps[:, 2:4, :].rearrange("p b n -> p (b n)")
        rowp = ps[0:1, 6, 256:512]
        shp = [ps[:, h, 0:TG * 96].rearrange("p (t g c) -> p t g c", t=TG, g=3) for h in range(2)]
        sp_ = ps[0:2, 0, :]
        accp = ps[:, 2:4, :]
        atp = [ps[:, 0, 0:D], ps[:, 1, 0:D]]
        cbp, nsqp = ps[:, 1, 256:258], ps[:, 1, 258:260]
        nbp = [ps[:, h, 384:512] for h in range(2)]
        midp = [ps[:, 2, :], ps[:, 3, :]]
        op = [ps[:, 4 + t // 2, (t % 2) * D:(t % 2 + 1) * D] for t in range(TB)]
        hp = [ps[0:H, s % BANKS, 0:P] for s in range(RING)]
        yp = [ps[:, BANKS + s % BANKS, 0:D] for s in range(RING)]

        x_v = x.rearrange("(t p) d -> p t d", p=P)
        out_v = out.rearrange("(t p) d -> p t d", p=P)
        xs_v = xs_dram.rearrange("(t p) d -> p t d", p=P)
        y_v = y_dram.rearrange("(i p) d -> p i d", p=P)
        ROUNDS = ITEMS // RING
        HALF = RING // 2

        def group(b, h):
            return bass.ds(b * TB + h * TG, TG)

        block = ctx.enter_context(nc.Block())

        @block.sync
        def _(sync):
            for free in (*o_ps, *xst_ps, *y_ps, *y_ok):
                sync.sem_inc(free, CREDIT)
            for g in range(TILES // TG):
                if g:
                    sync.wait_ge(x_in, 16 * g)
                sync.dma_start(x_all[:, g * TG:(g + 1) * TG, :], x_v[:, g * TG:(g + 1) * TG, :]).then_inc(x_in, 16)

            with sync.Fori(0, BATCHES) as b:
                for h in range(2):
                    sync.wait_ge(xn_ok[h], CREDIT + b + 1)
                    sync.dma_start(xn_all[:, group(b, h), :], xn_s[:, h]).then_inc(xn_kept[h], 16)
                for h in range(2):
                    sync.wait_ge(xt_ok[h], CREDIT + b + 1)
                    sync.dma_start(xt_all[:, b * 2 + h], xt_s[:, h]).then_inc(xt_kept[h], 16)

            def back(b, h):
                sync.wait_ge(o_ps[h], CREDIT + b)
                sync.dma_start(xt_s[:, h], xt_all[:, b * 2 + h]).then_inc(xt_back[h], 16)
                sync.dma_start(xn_s[:, h], xn_all[:, group(b, h), :]).then_inc(xn_back[h], 16)

            for h in range(2):
                sync.wait_ge(xn_kept[h], CREDIT + 16 * BATCHES)
                sync.wait_ge(xt_kept[h], CREDIT + 16 * BATCHES)
                sync.wait_ge(lg_ps[h], CREDIT + BATCHES)
            with sync.Fori(0, 2) as b:
                for h in range(2):
                    back(b, h)

            def load_weights(i, s):
                expert = sync.value_load(item_row[0:1, bass.ds(i * RING + s, 1)], min_val=0, max_val=E - 1)
                sync.wait_ge(y_ps[s], CREDIT + i)
                sync.dma_start(w_s[:, s], wx[bass.ds(expert, 1)].rearrange("e p c -> p (e c)")).then_inc(w_in[s], 16)

            def store_half(i, q):
                for s in range(q * HALF, (q + 1) * HALF):
                    sync.wait_ge(y_ok[s], CREDIT + i + 1)
                sync.dma_start(y_v[:, bass.ds(i * RING + q * HALF, HALF), :], y_s[:, q * HALF:(q + 1) * HALF, :]).then_inc(y_out[q], 16)

            sync.wait_ge(row_ok, 1)
            for s in range(RING):
                load_weights(0, s)
            sync.wait_ge(scattered, 16 * TILES)
            with sync.Fori(0, BATCHES) as b:
                for h in range(2):
                    sync.wait_ge(o_ps[h], CREDIT + 2)
                    sync.wait_ge(xst_ps[h], CREDIT + b)
                    sync.dma_start(xs_s[:, h], xs_v[:, group(b, h), :]).then_inc(xs_in[h], 16)
            for h in range(2):
                sync.wait_ge(xst_ps[h], CREDIT + BATCHES)
                back(2, h)
            with sync.Fori(1, ROUNDS) as i:
                for q in range(2):
                    for s in range(q * HALF, (q + 1) * HALF):
                        load_weights(i, s)
                    store_half(i - 1, q)
            for q in range(2):
                store_half(ROUNDS - 1, q)
            for h in range(2):
                back(3, h)
            for g in range(TILES // TG):
                for t in range(g * TG, (g + 1) * TG):
                    sync.wait_ge(added[t % QUEUE], 16 * (t // QUEUE + 1))
                sync.dma_start(out_v[:, g * TG:(g + 1) * TG, :], x_all[:, g * TG:(g + 1) * TG, :]).then_inc(stored, 16)
            sync.wait_ge(stored, 16 * (TILES // TG))

        @block.gpsimd
        def _(pool):
            clear = [(h_s[H:H + 1], 1.0),
                     (zero[:], 0.0), (p_all[:, :, 0], 0.0), (e_all[:, :, TB], 0.0), (qe[:, :, 0, R:], 0.0),
                     (macc[:, :, :, 0:1], 0.0), (sraw[:, :, 0:1], 0.0), (reset2[:], 1.0),
                     (reset2[:, :, 0:1], 0.0), (reset[:], 1.0), (reset[:, :, 0:1], 0.0), (ones_bf[:], 1.0)]
            for i, (what, value) in enumerate(clear):
                nc.gpsimd.memset(what, value).then_inc(pad_ok, 1)
                pool.wait_ge(pad_ok, i + 1)
            pool.wait_ge(early_in, 16)
            pool.wait_ge(late_in, 16)
            made = [nc.gpsimd.tensor_scalar(wpgt[:, k], wpt[:, k], gb[:, k, 0:1], None, ALU.mult) for k in range(KH)]
            made += [nc.gpsimd.tensor_scalar(gbn[:, :, 0], gb[:, :, 0], -1.0, None, ALU.mult),
                     nc.gpsimd.tensor_copy(gbn[:, :, 1], gb[:, :, 1]),
                     nc.gpsimd.tensor_scalar(at2[:], col["atrep"], SCALING, None, ALU.mult),
                     nc.gpsimd.tensor_copy(ntri_bf[:], col["ntri"])]
            for m in made:
                m.then_inc(made_ok, 1)
            pool.wait_ge(place_ok, 1)
            for h in range(2):
                pool.wait_ge(xn_kept[h], CREDIT + 16 * BATCHES)
            for t in range(TILES):
                pool.indirect_dma_start(xs_dram, bass.IndirectOffsetOnAxis(vi[:, 1, t:t + 1], axis=0),
                                        xn_all[:, t, :], None).then_inc(scattered, 16)
            for h in range(2):
                pool.wait_ge(o_ps[h], CREDIT + 2)
            nc.gpsimd.memset(xst[:, :, N:], 0.0).then_inc(pad_ok, 1)
            for q in range(2):
                pool.wait_ge(y_out[q], CREDIT + 16 * ROUNDS)
            for t in range(TILES):
                if t % TG == 0:
                    pool.wait_ge(o_read[t // TG % 2], CREDIT + t // TB + 1)
                if t >= QUEUE:
                    pool.wait_ge(added[t % QUEUE], 16 * (t // QUEUE))
                pool.indirect_dma_start(x_all[:, t, :], None, y_dram, bass.IndirectOffsetOnAxis(vi[:, 3, t:t + 1], axis=0),
                                        compute_op=ALU.add).then_inc(added[t % QUEUE], 16)

        @block.scalar
        def _(act):
            for free in (*xn_kept, *tr_ps, *xt_kept, *lg_ps, sh_ps, acc_ok, cb_ok):
                act.sem_inc(free, CREDIT)
            act.dma_start(e_sb[:], early).then_inc(early_in, 16)
            act.wait_ge(early_in, 16)
            act.dma_start(l_sb[:], late).then_inc(late_in, 16)

            def deviation(b):
                act.wait_ge(var_ok, b + 1)
                nc.scalar.activation(nrm[:, 1], nrm[:, 0], ACT.Sqrt).then_inc(dev_ok, 1)

            def normalise(b):
                act.wait_ge(nr_ok, b + 1)
                for h in range(2):
                    act.wait_ge(xn_kept[h], CREDIT + 16 * b)
                    act.wait_ge(tr_ps[h], CREDIT + b)
                    for t in range(TG):
                        at = b * TB + h * TG + t
                        last = nc.scalar.activation(xn_s[:, h, t], x_all[:, at], ACT.Identity,
                                                    bias=nr[:, 1, bass.ds(at, 1)], scale=nr[:, 0, bass.ds(at, 1)],
                                                    accum_out=sums[:, 0, bass.ds(at, 1)])
                    last.then_inc(xn_ok[h], 1)

            def evacuate(b, then):
                for h in range(2):
                    act.wait_ge(tr_ps[h], CREDIT + b + 1)
                    act.wait_ge(xt_kept[h], CREDIT + 16 * b)
                    act.wait_ge(lg_ps[h], CREDIT + b)
                    nc.scalar.activation(xt_s[:, h], tr[h], ACT.Copy).then_inc(xt_ok[h], 1)
                then()
                for h in range(2):
                    act.wait_ge(lg_read[h], b + 1)
                    nc.scalar.activation(e_raw[:, group(b, h), :], lgp[h][:, :, E:E + R], ACT.Copy)
                    nc.scalar.activation(p_all[:, b, bass.ds(h * TG + 1, TG), :], lgp[h][:, :, E + R:], ACT.Copy).then_inc(ep_ok[h], 1)

            act.wait_ge(pad_ok, CLEARED)
            deviation(0)
            normalise(0)
            with act.Fori(0, BATCHES - 1) as b:
                deviation(b + 1)
                evacuate(b, lambda: normalise(b + 1))
            evacuate(BATCHES - 1, lambda: None)
            act.wait_ge(g1_ps, 1)
            nc.scalar.activation(g1b1[:], g1p, ACT.Copy)
            nc.scalar.activation(ws[:], wsp, ACT.Copy).then_inc(g1_ok, 1)
            for h in range(2):
                act.wait_ge(xn_kept[h], CREDIT + 16 * BATCHES)
            act.sem_inc(sq_ok, CREDIT)
            with act.Fori(0, TILES // 4) as g:
                act.wait_ge(sq_ok, CREDIT + g)
                for t in range(4):
                    last = nc.scalar.activation(junk[:, t], xn_all[:, g * 4 + t], ACT.Square, accum_out=sums[:, 1, bass.ds(g * 4 + t, 1)])
                last.then_inc(sq_ok, 1)
            act.wait_ge(v2_ok, 1)
            nc.scalar.activation(ms[:, :, 1], tmp2[:, 2], ACT.Sqrt).then_inc(sd2_ok, 1)

            def stage2(first):
                with act.Fori(first, first + 2) as b:
                    for h in range(2):
                        act.wait_ge(q_ok, 2 * b + h + 1)
                        nc.scalar.activation(qe[:, h * TG:(h + 1) * TG, 1:3, R:], shp[h][:, :, 1:3, R:], ACT.Copy).then_inc(e_ok, 1)
                    act.wait_ge(acc_ps, CREDIT + b + 1)
                    act.wait_ge(acc_ok, CREDIT + b)
                    for k in range(KH):
                        nc.scalar.activation(macc[:, k, :, 1:], accp[:, k, 0:(CB - 1) * 2 * R].rearrange("p (c r) -> p r c", r=2 * R), ACT.Copy)
                    nc.scalar.activation(sraw[:, :, 1:], sp_[:, 0:(CB - 1) * 2 * R].rearrange("p (c r) -> p r c", r=2 * R)[:, 0:R, :],
                                         ACT.Copy).then_inc(macc_ok, 1)
                    act.wait_ge(acc_ok, CREDIT + b + 1)
                    for k in range(KH):
                        nc.scalar.activation(accm[:, k].rearrange("p h (r c) -> p h r c", c=CG),
                                             acc[:, k, 0:R, :].rearrange("p r (h c) -> p h r c", c=CG), ACT.Copy)
                    nc.scalar.activation(saccm[:].rearrange("p h (r c) -> p h r c", c=CG),
                                         sacc[:].rearrange("p r (h c) -> p h r c", c=CG), ACT.Copy).then_inc(accm_ok, 1)
                    for h in range(2):
                        act.wait_ge(at_ps, 2 * b + h + 1)
                        act.wait_ge(cb_ok, CREDIT + b)
                        nc.scalar.activation(sqa[:, h], atp[h], ACT.Square, accum_out=cols[:, 0, h:h + 1]).then_inc(sqa_ok, 1)
                    act.wait_ge(nsq_ok, b + 1)
                    nc.scalar.activation(cols[:, 3], cols[:, 2], ACT.Sqrt, scale=LR * LR).then_inc(tn_ok, 1)

            stage2(0)
            with act.Fori(0, BATCHES) as b:
                for h in range(2):
                    act.wait_ge(xst_ps[h], CREDIT + b + 1)
                    nc.scalar.activation(xst[:, 1, bass.ds((b * 2 + h) * GT, GT)], tr[h][:, 1], ACT.Copy).then_inc(xst_ok[h], 1)
            with act.Fori(0, ROUNDS) as i:
                for s in range(RING):
                    act.wait_ge(h_ps[s], i + 1)
                    nc.scalar.activation(h_s[0:H, s], hp[s], ACT.Relu, bias=w_s[0:H, s, KH * H:KH * H + 1]).then_inc(h_ok[s], 1)
            stage2(2)

        @block.vector
        def _(dve):
            for free in (*xn_ok, acc_ps, *y_out):
                dve.sem_inc(free, CREDIT)
            vec = nc.vector
            n = Count(0)

            def mine(instruction):
                instruction.then_inc(dv, 1)
                dve.wait_ge(dv, n())

            def norm(b):
                for t in range(TB):
                    if t % TG == 0:
                        dve.wait_ge(x_in, 16 * (2 * b + t // TG + 1))
                    last = vec.bn_stats(stats[:, t], x_all[:, b * TB + t])
                last.then_inc(dv, 1)
                dve.wait_ge(dv, n())
                vec.memset(spare[:], 0.0)
                for t in range(TB):
                    last = vec.bn_aggr(mv[:, t], stats[:, t])
                mine(last)
                vec.tensor_scalar(nrm[:, 0], mv[:, :, 1], EPS, None, ALU.add).then_inc(var_ok, 1)
                dve.wait_ge(dev_ok, b + 1)
                mine(vec.reciprocal(nrm[:, 2], nrm[:, 1]))
                mine(vec.tensor_tensor(nrm[:, 3], nrm[:, 2], nrm[:, 2], ALU.mult))
                mine(vec.tensor_tensor(nrm[:, 3], nrm[:, 3], nrm[:, 0], ALU.mult))
                mine(vec.tensor_scalar(nrm[:, 3], nrm[:, 3], -0.5, 1.5, ALU.mult, ALU.add))
                now = bass.ds(b * TB, TB)
                mine(vec.tensor_tensor(nr[:, 0, now], nrm[:, 2], nrm[:, 3], ALU.mult))
                vec.scalar_tensor_tensor(nr[:, 1, now], mv[:, :, 0], -1.0, nr[:, 0, now], ALU.mult, ALU.mult).then_inc(nr_ok, 1)

            def choose(b, h):
                dve.wait_ge(lg_ps[h], CREDIT + b + 1)
                rb = col["rb"].unsqueeze(1).broadcast_to([P, TG, E])
                vec.tensor_tensor(lg[:, h, 0], lgp[h][:, :, 0:E], rb, ALU.add).then_inc(lg_read[h], 1)
                dve.wait_ge(lg_read[h], b + 1)
                mine(vec.tensor_reduce(best[:, h, 0], lg[:, h, 0], AX.X, ALU.max))
                b0 = best[:, h, 0].unsqueeze(2).broadcast_to([P, TG, E])
                mine(vec.tensor_tensor(lg[:, h, 1], lg[:, h, 0], b0, ALU.is_ge))
                mine(vec.tensor_tensor(lg[:, h, 2], lg[:, h, 1], edesc.unsqueeze(1).broadcast_to([P, TG, E]), ALU.mult))
                mine(vec.tensor_reduce(best[:, h, 1], lg[:, h, 2], AX.X, ALU.max))
                b1 = best[:, h, 1].unsqueeze(2).broadcast_to([P, TG, E])
                vec.tensor_tensor(oh_all[:, :, group(b, h)].rearrange("p e t -> p t e"), lg[:, h, 2], b1, ALU.is_equal).then_inc(oh_ok[h], 1)

            norm(0)
            dve.wait_ge(early_in, 16)
            dve.wait_ge(wa_ps, 1)
            for k in range(KH):
                vec.tensor_scalar(w64[:, k, E:E + R], wa[:, k], gb[:, k, 0:1], None, ALU.mult)
                last = vec.tensor_scalar(bwa[:, k], wa[:, k], gb[:, k, 1:2], None, ALU.mult)
            last.then_inc(w64_ok, 1)
            start, steps = n.k, 15
            with dve.Fori(0, BATCHES - 1) as b:
                n = Count(start + b * steps)
                norm(b + 1)
                choose(b, 0)
                choose(b, 1)
                assert n.k == steps, n.k
            n = Count(start + (BATCHES - 1) * steps)
            choose(BATCHES - 1, 0)
            choose(BATCHES - 1, 1)

            flat = lambda t: t.rearrange("p e t -> p (e t)")
            tiles, cn, ct, off, dist, pack, cmp, sel = (rt[:, i] for i in range(8))
            carry = reset2[:].rearrange("p a c -> p (a c)")
            dve.wait_ge(rank_ps, 1)
            mine(vec.tensor_tensor_scan(flat(cin[:]), flat(reset[:]), total, 0.0, ALU.mult, ALU.add))
            vec.tensor_tensor(flat(place[:]), rank, flat(cin[:]), ALU.add).then_inc(dv, 1)
            num = cin[:, :, TILES - 1]
            vec.tensor_scalar(qi[:], num, float(P - 1), None, ALU.add).then_inc(dv, 1)
            dve.wait_ge(dv, n(2))
            mine(vec.tensor_scalar(qi[:], qi[:], 7, 7, ALU.arith_shift_right, ALU.logical_shift_left))
            mine(vec.tensor_copy(tiles, qi[:]))
            always = col["ones"][:, 0:E]
            vec.tensor_tensor_scan(cn, always, num, 0.0, ALU.mult, ALU.add).then_inc(dv, 1)
            vec.tensor_tensor_scan(ct, always, tiles, 0.0, ALU.mult, ALU.add).then_inc(dv, 1)
            dve.wait_ge(dv, n(2))
            mine(vec.tensor_tensor(off, cn, num, ALU.subtract))
            mine(vec.tensor_tensor(dist, ct, tiles, ALU.subtract))
            mine(vec.tensor_tensor(dist, dist, off, ALU.subtract))
            mine(vec.scalar_tensor_tensor(pack, dist, float(PK), off, ALU.mult, ALU.add))
            mine(vec.tensor_tensor(place[:], place[:], pack.unsqueeze(2).broadcast_to([P, E, TILES]), ALU.add))
            mine(vec.tensor_tensor(place[:], place[:], oh_all[:], ALU.mult))
            mine(vec.tensor_reduce(tmp2[:, 0], place[:].rearrange("p e t -> p t e"), AX.X, ALU.add))
            mine(vec.tensor_copy(vi[:, 0], tmp2[:, 0]))
            vec.tensor_scalar(vi[:, 1], vi[:, 0], PK - 1, None, ALU.bitwise_and).then_inc(place_ok, 1)
            vec.tensor_scalar(vi[:, 2], vi[:, 0], 12, None, ALU.arith_shift_right).then_inc(dv, 1)
            dve.wait_ge(dv, n())
            dve.wait_ge(place_ok, 1)
            vec.tensor_tensor(vi[:, 3], vi[:, 1], vi[:, 2], ALU.add)
            mine(vec.tensor_scalar(cmp, ct, icol, None, ALU.is_le))
            mine(vec.tensor_reduce(item[:, 2:3], cmp, AX.X, ALU.add))
            mine(vec.tensor_scalar(item[:, 0:1], item[:, 2:3], float(E - 1), None, ALU.min))
            mine(vec.scalar_tensor_tensor(sel, eiota, item[:, 0:1], dist, ALU.is_equal, ALU.mult))
            mine(vec.tensor_reduce(item[:, 3:4], sel, AX.X, ALU.add))
            mine(vec.tensor_tensor(item[:, 2:3], icol, item[:, 3:4], ALU.subtract))
            vec.tensor_scalar(item[:, 1:2], item[:, 2:3], float(N), None, ALU.min).then_inc(item_ok, 1)

            dve.wait_ge(sq_ok, CREDIT + TILES // 4)
            vec.tensor_scalar(ms[:, :, 0], sums[:, 0], 1.0 / D, None, ALU.mult).then_inc(dv, 1)
            vec.tensor_scalar(tmp2[:, 0], sums[:, 1], 1.0 / D, EPS, ALU.mult, ALU.add).then_inc(dv, 1)
            dve.wait_ge(dv, n(2))
            mine(vec.tensor_tensor(tmp2[:, 1], ms[:, :, 0], ms[:, :, 0], ALU.mult))
            vec.tensor_tensor(tmp2[:, 2], tmp2[:, 0], tmp2[:, 1], ALU.subtract).then_inc(v2_ok, 1)
            dve.wait_ge(sd2_ok, 1)
            mine(vec.reciprocal(r2[:, 0], ms[:, :, 1]))
            mine(vec.scalar_tensor_tensor(r2[:, 1], ms[:, :, 0], -1.0, r2[:, 0], ALU.mult, ALU.mult))
            wide = lambda v: v.unsqueeze(2).broadcast_to([P, TILES, R])
            same = lambda v: v.unsqueeze(1).broadcast_to([P, TILES, R])
            e_in = e_raw[:]
            dve.wait_ge(g1_ok, 1)
            vec.tensor_tensor(e_in, e_in, wide(r2[:, 0]), ALU.mult).then_inc(dv, 1)
            vec.tensor_tensor(tmp_e, wide(r2[:, 1]), same(g1b1[:, 0]), ALU.mult).then_inc(dv, 1)
            dve.wait_ge(dv, n(2))
            mine(vec.tensor_tensor(tmp_e, e_in, tmp_e, ALU.add))
            vec.tensor_tensor(e_all[:, :, 0:TB], tmp_e.rearrange("p (b t) r -> p b t r", b=BATCHES),
                              g1b1[:, 1].unsqueeze(1).unsqueeze(1).broadcast_to([P, BATCHES, TB, R]), ALU.add).then_inc(eb_ok, 1)
            dve.wait_ge(item_ps, 1)
            vec.tensor_copy(item_row[:], rowp).then_inc(row_ok, 1)

            def stage2(first, start, per):
                with dve.Fori(first, first + 2) as b:
                    nonlocal n
                    n = Count(start + (b - first) * per)
                    dve.wait_ge(acc_ps, CREDIT + b)
                    vec.tensor_copy(ms_b[:], ms[:, bass.ds(b * TB, TB), :])
                    for h in range(2):
                        dve.wait_ge(sh_ps, CREDIT + 2 * b + h + 1)
                        for g in range(3):
                            last = vec.tensor_tensor(qe[:, h * TG:(h + 1) * TG, g, 0:R], shp[h][:, :, g, 0:R],
                                                     r2[:, 0, group(b, h)].unsqueeze(2).broadcast_to([P, TG, R]), ALU.mult)
                        last.then_inc(q_ok, 1)
                    dve.wait_ge(macc_ok, b + 1)
                    vec.tensor_tensor_scan(acc.rearrange("p k r c -> p (k r c)"), carry,
                                           macc[:].rearrange("p k r c -> p (k r c)"), 0.0, ALU.mult, ALU.add)
                    vec.tensor_tensor_scan(sacc[:].rearrange("p r c -> p (r c)"), carry[0:2, 0:R * CB],
                                           sraw[:].rearrange("p r c -> p (r c)"), 0.0, ALU.mult, ALU.add).then_inc(acc_ok, 1)
                    dve.wait_ge(acc_ok, CREDIT + b + 1)
                    for h in range(2):
                        for k in range(KH):
                            v = acc[:, k, R:, h * CG:(h + 1) * CG]
                            last = vec.tensor_tensor(sqb[:, h, k].rearrange("p (r c) -> p r c", c=CG), v, v, ALU.mult)
                    last.then_inc(sqb_ok, 1)
                    dve.wait_ge(cb_ps, b + 1)
                    dve.wait_ge(sqa_ok, 2 * b + 2)
                    vec.tensor_tensor(cols[:, 1], cbp, cols[:, 0], ALU.add).then_inc(cb_ok, 1)
                    dve.wait_ge(nsq_ps, b + 1)
                    vec.tensor_scalar(cols[:, 2], nsqp, 1e-30, None, ALU.max).then_inc(nsq_ok, 1)
                    dve.wait_ge(tn_ok, b + 1)
                    mine(vec.tensor_scalar(cols[:, 4], cols[:, 3], 1e-6, None, ALU.add))
                    mine(vec.reciprocal(cols[:, 5], cols[:, 4]))
                    mine(vec.tensor_scalar(cols[:, 4], cols[:, 5], 1.0, -LR, ALU.min, ALU.mult))
                    mine(vec.tensor_scalar(cols[:, 5], cols[:, 4], SCALING, None, ALU.mult))
                    for h in range(2):
                        vec.tensor_scalar(dnb[:, h], ident, cols[:, 4, h:h + 1], None, ALU.mult)
                    for h in range(2):
                        last = vec.scalar_tensor_tensor(aeff[:, h], atp[h], cols[:, 5, h:h + 1], at2[:], ALU.mult, ALU.add)
                    last.then_inc(aeff_ok, 1)
                    for h in range(2):
                        dve.wait_ge(nb_ps, 2 * b + h + 1)
                        for k in range(KH):
                            vec.tensor_tensor(beff[:, h, k].rearrange("p (r c) -> p r c", c=CG), acc[:, k, R:, h * CG:(h + 1) * CG],
                                              nbp[h].rearrange("p (r c) -> p r c", c=CG), ALU.mult).then_inc(dv, 1)
                        dve.wait_ge(dv, n(2))
                        vec.tensor_tensor(beff[:, h], beff[:, h], btrep, ALU.add).then_inc(beff_ok, 1)
                    for h in range(2):
                        dve.wait_ge(mid_ps, 2 * b + h + 1)
                        vec.tensor_tensor(midm[:, h], midp[h], diag, ALU.mult).then_inc(mid_ok, 1)
                    for h in range(2):
                        dve.wait_ge(o_ps[h], CREDIT + b + 1)
                        for q in range(TG // 2):
                            t = h * TG + 2 * q
                            xo = x_all[:, bass.ds(b * TB + t, 2), :]
                            last = vec.tensor_tensor(xo, ps[:, 4 + t // 2, :].rearrange("p (t d) -> p t d", t=2), xo, ALU.add)
                        last.then_inc(o_read[h], 1)
                    assert n.k == per, n.k
                return start + 2 * per

            after = stage2(0, n.at + n.k, 8)
            with dve.Fori(0, BATCHES) as b:
                for h in range(2):
                    dve.wait_ge(xst_ps[h], CREDIT + b + 1)
                    vec.tensor_copy(xst[:, 0, bass.ds((b * 2 + h) * GT, GT)], tr[h][:, 0]).then_inc(xst_ok[h], 1)
            dve.wait_ge(scattered, 16 * TILES)
            for h in range(2):
                dve.wait_ge(xn_back[h], 32)
            with dve.Fori(0, ROUNDS) as i:
                for s in range(RING):
                    dve.wait_ge(y_ps[s], CREDIT + i + 1)
                    if s % HALF == 0:
                        dve.wait_ge(y_out[s // HALF], CREDIT + 16 * i)
                    vec.tensor_scalar(y_s[:, s], yp[s], 0.0, None, ALU.max).then_inc(y_ok[s], 1)
            stage2(2, after, 8)

        @block.tensor
        def _(pe):
            for free in (*xt_ok, *oh_ok, *ep_ok, beff_ok, *o_read, mid_ok, *xst_ok, *h_ok):
                pe.sem_inc(free, CREDIT)
            mm = nc.tensor.matmul
            pe.wait_ge(early_in, 16)
            for m in range(KH):
                for k in range(KH):
                    last = mm(wa[:, m], wp[:, k, m * P:(m + 1) * P], a_w[:, k], start=(k == 0), stop=(k == KH - 1))
            last.then_inc(wa_ps, 1)

            def transpose_group(h, source, done):
                for t in range(TG):
                    for k in range(KH):
                        last = nc.tensor.transpose(tr[h][:, k, t * P:(t + 1) * P], source[:, h, t, k * P:(k + 1) * P], ident)
                last.then_inc(done, 1)

            with pe.Fori(0, BATCHES) as b:
                for h in range(2):
                    pe.wait_ge(xn_ok[h], CREDIT + b + 1)
                    pe.wait_ge(xt_ok[h], CREDIT + b)
                    transpose_group(h, xn_s, tr_ps[h])
                pe.wait_ge(w64_ok, 1)
                for h in range(2):
                    pe.wait_ge(xt_ok[h], CREDIT + b + 1)
                    pe.wait_ge(oh_ok[h], CREDIT + b)
                    pe.wait_ge(ep_ok[h], CREDIT + b)
                    for t in range(TG):
                        for k in range(KH):
                            last = mm(lgp[h][:, t], xt_s[:, h, k, t * P:(t + 1) * P], w64[:, k], start=(k == 0), stop=(k == KH - 1))
                    last.then_inc(lg_ps[h], 1)
            pe.wait_ge(made_ok, MADE)
            for k in range(KH):
                mm(g1p[:, 0], ones, w64[:, k, E:E + R], start=(k == 0), stop=(k == KH - 1))
            for k in range(KH):
                mm(g1p[:, 1], ones, bwa[:, k], start=(k == 0), stop=(k == KH - 1))
            for k in range(KH):
                last = mm(wsp, gbn[:, k], wpt[:, k], start=(k == 0), stop=(k == KH - 1))
            last.then_inc(g1_ps, 1)
            pe.wait_ge(pad_ok, CLEARED)
            for h in range(2):
                pe.wait_ge(oh_ok[h], CREDIT + BATCHES)
                pe.wait_ge(xt_ok[h], CREDIT + BATCHES)
            oh = oh_all[:].rearrange("p e t -> p (e t)")
            for c in range(2):
                mm(total[:, c * 512:(c + 1) * 512], ones_bf[:], oh[:, c * 512:(c + 1) * 512], start=True, stop=True)
            for c in range(2):
                last = mm(rank[:, c * 512:(c + 1) * 512], ntri_bf[:], oh[:, c * 512:(c + 1) * 512], start=True, stop=True)
            last.then_inc(rank_ps, 1)

            def base(b, tiles):
                for t in tiles:
                    h = t // TG
                    if t % TG == 0:
                        pe.wait_ge(xt_back[h], 16 * (b + 1))
                    if t % 2 == 0:
                        pe.wait_ge(o_read[h], CREDIT + b)
                    for k in range(KH):
                        mm(op[t], xt_s[:, h, k, (t % TG) * P:(t % TG + 1) * P], wbt[:, k], start=(k == 0 and t % 2 == 0), stop=False)

            def stage2(first):
                with pe.Fori(first, first + 2) as b:
                    base(b, range(0, 4))
                    pe.wait_ge(eb_ok, 1)
                    pe.wait_ge(beff_ok, CREDIT + 2 * b)
                    for h in range(2):
                        t0, t1 = h * TG, (h + 1) * TG
                        p_b, e_b = p_all[:, b], e_all[:, b]
                        mm(shp[h][:, :, 0, 0:R], shift[0], p_b[:, t0:t1], start=True, stop=False)
                        mm(shp[h][:, :, 1, 0:R], shift[1], p_b[:, t0 + 1:t1 + 1], start=False, stop=False)
                        mm(shp[h][:, :, 2, 0:R], shift[2], p_b[:, t0 + 1:t1 + 1], start=False, stop=False)
                        mm(shp[h][:, :, 1, R:], shift[3], e_b[:, t0:t1], start=False, stop=False)
                        mm(shp[h][:, :, 2, R:], shift[4], e_b[:, t0:t1], start=False, stop=False)
                        mm(shp[h][:, :, 2, R:], shift[5], e_b[:, t0 + 1:t1 + 1], start=False, stop=True).then_inc(sh_ps, 1)
                    pe.wait_ge(mid_ok, CREDIT + 2 * b)
                    for k in range(KH):
                        mm(accp[:, k], zero[:, 0:P], zero[:, 0:512], start=True, stop=False)
                    pe.wait_ge(q_ok, 2 * b + 2)
                    pe.wait_ge(e_ok, 2 * b + 2)
                    mm(sp_, zero[:, 0:2], zero[:, 0:512], start=True, stop=False)
                    for t in range(TB):
                        if t % TG == 0:
                            pe.wait_ge(xn_back[t // TG], 16 * (b + 1))
                        g = 1 if t == 0 else 0
                        rhs = qe[:, t, g:]
                        cols_ = slice((2 * t - 1 + g) * 2 * R, (2 * t + 2) * 2 * R)
                        for k in range(KH):
                            mm(accp[:, k, cols_], xn_s[:, t // TG, t % TG, k * P:(k + 1) * P], rhs, start=False, stop=(t == TB - 1))
                        last = mm(sp_[:, cols_], ms_b[:, t], rhs, start=False, stop=(t == TB - 1))
                    last.then_inc(acc_ps, 1)
                    base(b, range(4, 6))
                    pe.wait_ge(accm_ok, b + 1)
                    for h in range(2):
                        for k in range(KH):
                            mm(atp[h], accm[:, k, h], wpgt[:, k], start=(k == 0), stop=False)
                        mm(atp[h], saccm[:, h], ws[:], start=False, stop=True).then_inc(at_ps, 1)
                    pe.wait_ge(sqb_ok, b + 1)
                    pe.wait_ge(sqa_ok, 2 * b + 2)
                    for h in range(2):
                        for k in range(KH):
                            last = mm(cbp[:, h:h + 1], sqb[:, h, k], ones[:, 0:1], start=(k == 0), stop=(k == KH - 1))
                    last.then_inc(cb_ps, 1)
                    pe.wait_ge(cb_ok, CREDIT + b + 1)
                    mm(nsqp, blk, cols[:, 1], start=True, stop=True).then_inc(nsq_ps, 1)
                    base(b, range(6, 8))
                    pe.wait_ge(aeff_ok, b + 1)
                    for h in range(2):
                        mm(nbp[h], ones, dnb[:, h], start=True, stop=True).then_inc(nb_ps, 1)
                    for h in range(2):
                        pe.wait_ge(beff_ok, CREDIT + 2 * b + h + 1)
                        for k in range(KH):
                            last = mm(midp[h], beff[:, h, k], xt_s[:, h, k], start=(k == 0), stop=(k == KH - 1))
                        last.then_inc(mid_ps, 1)
                    for h in range(2):
                        pe.wait_ge(mid_ok, CREDIT + 2 * b + h + 1)
                        for t in range(TG):
                            last = mm(op[h * TG + t], midm[:, h, t * P:(t + 1) * P], aeff[:, h], start=False, stop=(t % 2 == 1))
                        last.then_inc(o_ps[h], 1)

            pe.wait_ge(item_ok, 1)
            for c in range(2):
                last = nc.tensor.transpose(rowp[:, c * P:(c + 1) * P], item[:, c:c + 1], ident)
            last.then_inc(item_ps, 1)
            pe.wait_ge(g1_ok, 1)
            pe.wait_ge(row_ok, 1)
            stage2(0)

            pe.wait_ge(mid_ok, CREDIT + 4)
            pe.wait_ge(aeff_ok, 2)
            with pe.Fori(0, BATCHES) as b:
                for h in range(2):
                    pe.wait_ge(xs_in[h], 16 * (b + 1))
                    pe.wait_ge(xst_ok[h], CREDIT + 2 * b)
                    transpose_group(h, xs_s, xst_ps[h])
            for h in range(2):
                pe.wait_ge(xst_ok[h], CREDIT + 2 * BATCHES)
            for h in range(2):
                pe.wait_ge(o_read[h], CREDIT + 2)
            pe.wait_ge(pad_ok, CLEARED + 1)

            def first_layer(i, s):
                first_token = pe.value_load(item_row[0:1, bass.ds(P + i * RING + s, 1)], min_val=0, max_val=N)
                pe.wait_ge(w_in[s], 16 * (i + 1))
                if s < BANKS:
                    pe.wait_ge(h_ok[s + BANKS], CREDIT + i)
                else:
                    pe.wait_ge(h_ok[s - BANKS], CREDIT + i + 1)
                for k in range(KH):
                    last = mm(hp[s], w_s[:, s, k * H:(k + 1) * H], xst[:, k, bass.ds(first_token, P)], start=(k == 0), stop=(k == KH - 1))
                last.then_inc(h_ps[s], 1)

            def second_layer(i, s):
                pe.wait_ge(h_ok[s], CREDIT + i + 1)
                if s < BANKS:
                    pe.wait_ge(y_ok[s + BANKS], CREDIT + i)
                else:
                    pe.wait_ge(y_ok[s - BANKS], CREDIT + i + 1)
                mm(yp[s], h_s[:, s], w_s[0:H + 1, s, KH * H + 1:], start=True, stop=True).then_inc(y_ps[s], 1)

            AHEAD = 2
            for s in range(AHEAD):
                first_layer(0, s)

            def one_round(i, last):
                for s in range(RING):
                    ahead = s + AHEAD
                    if ahead < RING:
                        first_layer(i, ahead)
                    elif not last:
                        first_layer(i + 1, ahead - RING)
                    second_layer(i, s)

            with pe.Fori(0, ROUNDS - 1) as i:
                one_round(i, False)
            one_round(ROUNDS - 1, True)
            for s in range(BANKS, RING):
                pe.wait_ge(y_ok[s], CREDIT + ROUNDS)
            stage2(2)


def kernel(L0_attn_x, L0_attn_Wb, L0_attn_init_A, L0_attn_init_B, L0_attn_ln_gamma, L0_attn_ln_beta, L0_attn_Wp,
           L0_ffn_router_w, L0_ffn_router_b, L0_ffn_weights1, L0_ffn_bias1, L0_ffn_weights2, L0_ffn_bias2):
    import numpy as np
    import concourse.bacc as bacc
    from concourse.bass_utils import run_bass_kernel_spmd

    f = lambda a: np.ascontiguousarray(np.asarray(a))
    halves = lambda a: f(a).reshape(KH, P, -1).transpose(1, 0, 2).reshape(P, -1)
    eye = np.eye(P, dtype=np.float32)
    k, m = np.arange(P)[:, None], np.arange(P)[None, :]
    shifts = [(k == P - 1) & (m == 0), (k == m - 1) & (m <= CHUNK), (k == m - 1) & (m > CHUNK),
              (k == m + 1) & (m < CHUNK), (k == m + 1) & (m >= CHUNK), (k == 0) & (m == P - 1)]
    router, b_t = f(L0_ffn_router_w).T, f(L0_attn_init_B).T
    parts = {
        "ident": eye,
        "w64": halves(np.concatenate([router, np.zeros((D, R), np.float32), b_t], 1)),
        "rb": np.tile(f(L0_ffn_router_b), (P, 1)),
        "edesc": np.tile(E - np.arange(E), (P, 1)),
        "wp": halves(L0_attn_Wp),
        "a": halves(L0_attn_init_A),
        "gb": halves(np.stack([f(L0_attn_ln_gamma), f(L0_attn_ln_beta)], 1)),
        "eiota": np.tile(np.arange(E), (P, 1)),
        "icol": P * np.arange(P)[:, None],
        "ones": np.ones((P, P)),
        "ntri": -1.0 * (k >= m),
        "sh": np.concatenate(shifts, 1),
        "blk": k % CG == m % CG,
        "diag": k % CG == np.arange(GT)[None, :] // CHUNK,
        "wpt": halves(f(L0_attn_Wp).T),
        "wbt": halves(f(L0_attn_Wb).T),
        "atrep": np.repeat(f(L0_attn_init_A).T, CG, 0),
        "btrep": halves(np.repeat(b_t, CG, 1)),
    }
    pack = lambda names: np.concatenate([parts[n].astype(np.float32) for n, _ in names], 1)
    w1 = f(L0_ffn_weights1).reshape(E, KH, P, H).transpose(0, 2, 1, 3).reshape(E, P, KH * H)
    below = lambda parts: np.concatenate([*parts, np.zeros((E, P - sum(p.shape[1] for p in parts), parts[0].shape[2]), np.float32)], 1)
    b1 = below([f(L0_ffn_bias1)[:, :, None]])
    w2 = below([f(L0_ffn_weights2), f(L0_ffn_bias2)[:, None, :]])
    arrays = {"x": f(L0_attn_x).reshape(N, D), "early": pack(EARLY), "late": pack(LATE), "wx": np.concatenate([w1, b1, w2], 2)}
    nc = bacc.Bacc("TRN2", target_bir_lowering=False, num_devices=1)
    args = [nc.dram_tensor(n, list(a.shape), F32, kind="ExternalInput").ap() for n, a in arrays.items()]
    out = nc.dram_tensor("out", [N, D], F32, kind="ExternalOutput").ap()
    build(nc, *args, out)
    got = run_bass_kernel_spmd(nc, [{n: np.ascontiguousarray(a) for n, a in arrays.items()}], core_ids=[0])
    return got.results[0]["out"].reshape(L0_attn_x.shape)
```

```python
from contextlib import ExitStack

import concourse.bass as bass
from concourse import mybir
from concourse.alu_op_type import AluOpType as ALU

F32 = mybir.dt.float32
BF16 = mybir.dt.bfloat16
I32 = mybir.dt.int32
ACT = mybir.ActivationFunctionType
AX = mybir.AxisListType

P = 128
D = 256
KH = D // P
N = 4096
TILES = N // P
BATCHES = 4
TB = TILES // BATCHES
TG = TB // 2
GT = TG * P
R = 16
CHUNK = 64
CB = TB * P // CHUNK
CG = CB // 2
E = 32
H = 64
ITEMS = 64
CREDIT = 1
CLEARED = 12
RING = 8
MADE = 6
BANKS = 4
EARLY_BASE = 3
STAGE_1_PAIRS = 3
QUEUE = 8
LR = 0.01 * 2.0
SCALING = 2.0
EPS = 1e-5
PK = 1 << 12

EARLY = [("ident", P), ("w64", KH * 64), ("rb", E), ("edesc", E), ("wp", KH * D), ("a", KH * R), ("gb", KH * 2)]
LATE = [("eiota", E), ("icol", 1), ("ones", P), ("ntri", P), ("sh", 6 * P), ("blk", P), ("diag", GT),
        ("wpt", KH * D), ("wbt", KH * D), ("atrep", D), ("btrep", KH * P)]


class Count:

    def __init__(self, at):
        self.at, self.k = at, 0

    def __call__(self, k=1):
        self.k += k
        return self.at + self.k


def build(nc, x, early, late, wx, out):
    ctx = ExitStack()
    with ctx:
        def sb(name, shape, dt=F32):
            return ctx.enter_context(nc.sbuf_tensor(name, shape, dt))

        def sem(name):
            return ctx.enter_context(nc.semaphore(name))

        def pair(name):
            return [sem(f"{name}{h}") for h in range(2)]

        xs_dram = nc.dram_tensor("xs_dram", [N, D], F32, kind="Internal").ap()
        y_dram = nc.dram_tensor("y_dram", [ITEMS * P, D], F32, kind="Internal").ap()

        e_sb = sb("e_sb", [P, sum(w for _, w in EARLY)])
        l_sb = sb("l_sb", [P, sum(w for _, w in LATE)])
        col = {}
        for t, names in ((e_sb, EARLY), (l_sb, LATE)):
            at = 0
            for n, w in names:
                col[n] = t[:, at:at + w]
                at += w
        ident, edesc, eiota, icol, ones, blk, diag = (col[k] for k in ("ident", "edesc", "eiota", "icol", "ones", "blk", "diag"))
        w64 = col["w64"].rearrange("p (k c) -> p k c", k=KH)
        wp = col["wp"].rearrange("p (k d) -> p k d", k=KH)
        a_w = col["a"].rearrange("p (k r) -> p k r", k=KH)
        gb = col["gb"].rearrange("p (k c) -> p k c", k=KH)
        wpt = col["wpt"].rearrange("p (k h) -> p k h", k=KH)
        wbt = col["wbt"].rearrange("p (k h) -> p k h", k=KH)
        btrep = col["btrep"].rearrange("p (k c) -> p k c", k=KH)
        shift = [col["sh"][:, i * P:(i + 1) * P] for i in range(6)]

        wpgt = sb("wpgt", [P, KH, D])
        gbn = sb("gbn", [P, KH, 2])
        ws = sb("ws", [2, D])
        bwa = sb("bwa", [P, KH, R])
        g1b1 = sb("g1b1", [P, 2, R])
        at2 = sb("at2", [P, D])
        ones_bf = sb("ones_bf", [P, P], BF16)
        ntri_bf = sb("ntri_bf", [P, P], BF16)
        reset2 = sb("reset2", [P, KH * 2 * R, CB])

        x_all = sb("x_all", [P, TILES, D])
        xn_all = sb("xn_all", [P, TILES, D])
        xt_all = sb("xt_all", [P, TILES // TG, KH, GT])
        aeff = sb("aeff", [P, 2, 2, D])
        beff = sb("beff", [P, 2, KH, P])
        xst = sb("xst", [P, KH, N + P])
        shared = xst[:].rearrange("p k n -> p (k n)")
        used = [0]

        def before_xst(shape):
            size = 1
            for w in shape[1:]:
                size *= w
            view = shared[0:shape[0], used[0]:used[0] + size]
            used[0] += size
            assert used[0] <= KH * (N + P)
            names = "abcd"[:len(shape) - 1]
            return view.rearrange(f"p ({' '.join(names)}) -> p {' '.join(names)}", **dict(zip(names, shape[1:])))

        e_raw = before_xst([P, TILES, R])
        e_all = sb("e_all", [P, BATCHES, TB + 1, R])
        p_all = sb("p_all", [P, BATCHES, TB + 1, R])
        nr = sb("nr", [P, 2, TILES])
        sums = sb("sums", [P, 2, TILES])
        ms = sb("ms", [P, TILES, 2])
        r2 = sb("r2", [P, 2, TILES])

        zero = sb("zero", [P, 512], BF16)
        stats = sb("stats", [P, TB, 6])
        mv = sb("mv", [P, TB, 2])
        nrm = sb("nrm", [P, 4, TB])
        lg = before_xst([P, 3, TB, E])
        oh_all = sb("oh_all", [P, E, TILES], BF16)
        best = sb("best", [P, 2, TB])

        cin = before_xst([P, E, TILES])
        place = before_xst([P, E, TILES])
        squares = shared[:, used[0] - 2 * E * TILES:used[0]].rearrange("p (t d) -> p t d", d=D)
        reset = before_xst([P, E, TILES])
        rt = before_xst([P, 10, E])
        qi = sb("qi", [P, E], I32)
        vi = sb("vi", [P, 4, TILES], I32)
        item = sb("item", [P, 4])
        item_row = sb("item_row", [1, 2 * P], I32)

        tmp2 = before_xst([P, 3, TILES])
        tmp_e = before_xst([P, TILES, R])
        qe = sb("qe", [P, TB, 3, 2 * R])
        macc = sb("macc", [P, KH, 2 * R, CB])
        acc = cin.rearrange("p (k a) (b c) -> p k (a b) c", k=KH, c=CB)
        sraw = sb("sraw", [2, R, CB])
        sacc = sb("sacc", [2, R, CB])
        accm = before_xst([P, KH, 2, P])
        sqb = before_xst([P, 2, KH, P])
        saccm = sb("saccm", [2, 2, P])
        sqa = before_xst([P, 2, D])
        cols = sb("cols", [P, 6, 2])
        dnb = before_xst([P, 2, P])
        midm = before_xst([P, 2, GT])

        WX = KH * H + 1 + D
        w_s = sb("w_s", [P, RING, WX])
        h_s = sb("h_s", [H + 1, RING, P])
        y_s = xn_all[:, 0:RING, :]
        SLOTS, ROOMS = 4, 6
        ACT_ALONE = 2
        xs_s = xn_all[:, 0:ROOMS * TG, :].rearrange("p (s t) d -> p s t d", s=ROOMS)

        ps = ctx.enter_context(nc.psum_tensor("ps", [P, 8, 512], F32))

        x_in = [sem(f"x_in{g}") for g in range(TILES // TG)]
        early_in, late_in = sem("early_in"), sem("late_in")
        dv = sem("dv")
        pad_ok, wa_ps, w64_ok, made_ok, g1_ps, g1_ok = (sem(n) for n in ("pad_ok", "wa_ps", "w64_ok", "made_ok", "g1_ps", "g1_ok"))
        var_ok, dev_ok, nr_ok, lg_ps, lg_read, ep_ok, oh_ok = (sem(n) for n in ("var_ok", "dev_ok", "nr_ok", "lg_ps", "lg_read", "ep_ok", "oh_ok"))
        xn_ok, tr_ps, xt_ok = pair("xn_ok"), pair("tr_ps"), pair("xt_ok")
        base_ps, base_added, counted = sem("base_ps"), sem("base_added"), sem("counted")
        rank_ps, item_ok, item_ps, place_ok, row_ok = (sem(n) for n in ("rank_ps", "item_ok", "item_ps", "place_ok", "row_ok"))
        scattered = sem("scattered")
        sq_ok, v2_ok, sd2_ok, eb_ok = sem("sq_ok"), sem("v2_ok"), sem("sd2_ok"), sem("eb_ok")
        sh_ps, q_ok, e_ok, acc_ps, macc_ok, acc_ok, accm_ok = (sem(n) for n in ("sh_ps", "q_ok", "e_ok", "acc_ps", "macc_ok", "acc_ok", "accm_ok"))
        at_ps, sqa_ok, sqb_ok, cb_ps, cb_ok, nsq_ps, nsq_ok = (sem(n) for n in ("at_ps", "sqa_ok", "sqb_ok", "cb_ps", "cb_ok", "nsq_ps", "nsq_ok"))
        tn_ok, nb_ps, beff_ok, aeff_ok, mid_ps, mid_ok = (sem(n) for n in ("tn_ok", "nb_ps", "beff_ok", "aeff_ok", "mid_ps", "mid_ok"))
        o_ps, o_read = pair("o_ps"), pair("o_read")
        xs_in = [sem(f"xs_in{g}") for g in range(TILES // TG)]
        xst_ps, xst_a, xst_v = sem("xst_ps"), sem("xst_a"), sem("xst_v")
        w_in, h_ps, h_ok, y_ps, y_ok = ([sem(f"{n}{s}") for s in range(RING)] for n in ("w_in", "h_ps", "h_ok", "y_ps", "y_ok"))
        y_out = pair("y_out")
        y_last = [sem(f"y_last{s}") for s in range(RING // 2)]
        added = [sem(f"added{s}") for s in range(QUEUE)]
        stored = sem("stored")

        tr = [ps[:, 2 * s:2 * s + 2, :] for s in range(SLOTS)]
        lgp = [ps[:, 4 + i, :].rearrange("p (t c) -> p t c", t=TB) for i in range(2)]
        wa = ps[:, 6, 0:KH * R].rearrange("p (k r) -> p k r", k=KH)
        g1p = ps[:, 7, 0:2 * R].rearrange("p (k r) -> p k r", k=2)
        wsp = ps[0:2, 7, 256:512]
        rank = ps[:, 4:6, :].rearrange("p b n -> p (b n)")
        total = ps[:, 6:8, :].rearrange("p b n -> p (b n)")
        rowp = ps[0:1, 7, 0:256]
        shp = [ps[:, h, 0:TG * 96].rearrange("p (t g c) -> p t g c", t=TG, g=3) for h in range(2)]
        sp_ = ps[0:2, 0, :]
        accp = ps[:, 2:4, :]
        atp = [ps[:, 0, 0:D], ps[:, 1, 0:D]]
        cbp, nsqp = ps[:, 1, 256:258], ps[:, 1, 258:260]
        nbp = [ps[:, 2 + h, 384:512] for h in range(2)]
        midp = [ps[:, 2, :], ps[:, 3, :]]
        midp = [midp, [ps[:, 6, :], ps[:, 7, :]]]
        pairp = [ps[:, 4 + q, :].rearrange("p (t d) -> p t d", t=2) for q in range(4)]

        def bank_of(pair):
            return 2 if pair < STAGE_1_PAIRS else (pair - STAGE_1_PAIRS) % 4 if pair <= TB else pair % 2

        op = [ps[:, 4 + t // 2, (t % 2) * D:(t % 2 + 1) * D] for t in range(TB)]
        hp = [ps[0:H, s % BANKS, 0:P] for s in range(RING)]
        yp = [ps[:, BANKS + s % BANKS, 0:D] for s in range(RING)]

        x_v = x.rearrange("(t p) d -> p t d", p=P)
        out_v = out.rearrange("(t p) d -> p t d", p=P)
        xs_v = xs_dram.rearrange("(t p) d -> p t d", p=P)
        y_v = y_dram.rearrange("(i p) d -> p i d", p=P)
        ROUNDS = ITEMS // RING
        HALF = RING // 2

        def group(b, h):
            return bass.ds(b * TB + h * TG, TG)

        GATHER_ORDER = [*range(2 * TB, TILES), *range(0, 2 * TB)]

        def gathered(t):
            at = GATHER_ORDER.index(t)
            return added[at % QUEUE], 16 * (at // QUEUE + 1)

        block = ctx.enter_context(nc.Block())

        @block.sync
        def _(sync):
            for free in (*y_ps, *y_ok):
                sync.sem_inc(free, CREDIT)
            for g in range(TILES // TG):
                sync.dma_start(x_all[:, g * TG:(g + 1) * TG, :], x_v[:, g * TG:(g + 1) * TG, :]).then_inc(x_in[g], 16)
                if g == 4:
                    sync.dma_start(l_sb[:], late).then_inc(late_in, 16)

            def experts_of(i):
                _, values = nc.values_load_multi_w_load_instructions(
                    item_row[0:1, bass.ds(i * RING, RING)], engines=[mybir.EngineType.SP], min_val=0, max_val=E - 1,
                    skip_runtime_bounds_check_because="the routing's minimum with E - 1 bounds them")
                return values

            def load_weights(i, s, expert):
                sync.wait_ge(y_ps[s], CREDIT + i)
                sync.dma_start(w_s[:, s], wx[bass.ds(expert, 1)].rearrange("e p c -> p (e c)")).then_inc(w_in[s], 16)

            def store_half(i, q):
                for s in range(q * HALF, (q + 1) * HALF):
                    sync.wait_ge(y_ok[s], CREDIT + i + 1)
                sync.dma_start(y_v[:, bass.ds(i * RING + q * HALF, HALF), :], y_s[:, q * HALF:(q + 1) * HALF, :]).then_inc(y_out[q], 16)

            sync.wait_ge(row_ok, 1)
            experts = experts_of(0)
            for s in range(RING):
                load_weights(0, s, experts[s])
            sync.wait_ge(scattered, 16 * TILES)
            sync.wait_ge(acc_ps, 2)
            for g in range(TILES // TG):
                if g == 4:
                    sync.wait_ge(acc_ps, 3)
                if g >= ROOMS:
                    sync.wait_ge(xst_ps, g - ROOMS + 1)
                sync.dma_start(xs_s[:, g % ROOMS], xs_v[:, g * TG:(g + 1) * TG, :]).then_inc(xs_in[g], 16)
            with sync.Fori(1, ROUNDS) as i:
                experts = experts_of(i)
                for q in range(2):
                    for s in range(q * HALF, (q + 1) * HALF):
                        load_weights(i, s, experts[s])
                    store_half(i - 1, q)
            store_half(ROUNDS - 1, 0)
            for s in range(HALF, RING):
                sync.wait_ge(y_ok[s], CREDIT + ROUNDS)
                sync.dma_start(y_v[:, ITEMS - RING + s:ITEMS - RING + s + 1, :], y_s[:, s:s + 1, :]).then_inc(y_last[s - HALF], 16)
            for g in (4, 5, 0, 1, 2, 6, 3, 7):
                if g < 4:
                    for t in range(g * TG, (g + 1) * TG):
                        sync.wait_ge(*gathered(t))
                else:
                    sync.wait_ge(o_read[g % 2], g // 2 + 1)
                sync.dma_start(out_v[:, g * TG:(g + 1) * TG, :], x_all[:, g * TG:(g + 1) * TG, :]).then_inc(stored, 16)
            sync.wait_ge(stored, 16 * (TILES // TG))

        @block.gpsimd
        def _(pool):
            clear = [(h_s[H:H + 1], 1.0),
                     (zero[:], 0.0), (p_all[:, :, 0], 0.0), (e_all[:, :, TB], 0.0), (qe[:, :, 0, R:], 0.0),
                     (macc[:, :, :, 0:1], 0.0), (sraw[:, :, 0:1], 0.0), (reset2[:], 1.0),
                     (reset2[:, :, 0:1], 0.0), (reset[:], 1.0), (reset[:, :, 0:1], 0.0), (ones_bf[:], 1.0)]
            for i, (what, value) in enumerate(clear):
                nc.gpsimd.memset(what, value).then_inc(pad_ok, 1)
                pool.wait_ge(pad_ok, i + 1)
            pool.wait_ge(early_in, 16)
            pool.wait_ge(late_in, 16)
            made = [nc.gpsimd.tensor_scalar(wpgt[:, k], wpt[:, k], gb[:, k, 0:1], None, ALU.mult) for k in range(KH)]
            made += [nc.gpsimd.tensor_scalar(gbn[:, :, 0], gb[:, :, 0], -1.0, None, ALU.mult),
                     nc.gpsimd.tensor_copy(gbn[:, :, 1], gb[:, :, 1]),
                     nc.gpsimd.tensor_scalar(at2[:], col["atrep"], SCALING, None, ALU.mult),
                     nc.gpsimd.tensor_copy(ntri_bf[:], col["ntri"])]
            for m in made:
                m.then_inc(made_ok, 1)
            pool.wait_ge(place_ok, 1)
            for t in range(TILES):
                pool.indirect_dma_start(xs_dram, bass.IndirectOffsetOnAxis(vi[:, 1, t:t + 1], axis=0),
                                        xn_all[:, t, :], None).then_inc(scattered, 16)
            pool.wait_ge(beff_ok, 6)
            for h in range(2):
                pool.wait_ge(o_ps[h], 2)
            nc.gpsimd.memset(xst[:, :, N:], 0.0).then_inc(pad_ok, 1)
            pool.wait_ge(y_out[0], CREDIT + 16 * ROUNDS)
            for last in y_last:
                pool.wait_ge(last, 16)
            for h in range(2):
                pool.wait_ge(o_read[h], 2)
            for at, t in enumerate(GATHER_ORDER):
                if at >= QUEUE:
                    pool.wait_ge(added[at % QUEUE], 16 * (at // QUEUE))
                pool.indirect_dma_start(x_all[:, t, :], None, y_dram, bass.IndirectOffsetOnAxis(vi[:, 3, t:t + 1], axis=0),
                                        compute_op=ALU.add).then_inc(added[at % QUEUE], 16)

        @block.scalar
        def _(act):
            act.dma_start(e_sb[:], early).then_inc(early_in, 16)

            def deviation(b):
                act.wait_ge(var_ok, b + 1)
                nc.scalar.activation(nrm[:, 1], nrm[:, 0], ACT.Sqrt).then_inc(dev_ok, 1)

            def keep_logits(b):
                act.wait_ge(lg_read, b + 1)
                nc.scalar.activation(e_raw[:, b * TB:(b + 1) * TB], lgp[b % 2][:, :, E:E + R], ACT.Copy)
                nc.scalar.activation(p_all[:, b, 1:], lgp[b % 2][:, :, E + R:], ACT.Copy).then_inc(ep_ok, 1)

            def keep_transposes(b, h):
                act.wait_ge(tr_ps[h], b + 1)
                nc.scalar.activation(xt_all[:, 2 * b + h, 1], tr[h][:, 1], ACT.Copy).then_inc(xt_ok[h], 1)

            def sum_squares(b, tiles):
                for t in tiles:
                    last = nc.scalar.activation(squares[:, t], xn_all[:, b * TB + t], ACT.Square, accum_out=sums[:, 1, b * TB + t:b * TB + t + 1])
                return last

            def second_deviation(b0, b1):
                act.wait_ge(v2_ok, 1 if b0 == 0 else 2)
                nc.scalar.activation(ms[:, b0 * TB:b1 * TB, 1], tmp2[:, 2, b0 * TB:b1 * TB], ACT.Sqrt).then_inc(sd2_ok, 1)

            deviation(0)
            for b in range(BATCHES):
                act.wait_ge(nr_ok, b + 1)
                for h in range(2):
                    for t in range(b * TB + h * TG, b * TB + (h + 1) * TG):
                        last = nc.scalar.activation(xn_all[:, t], x_all[:, t], ACT.Identity, bias=nr[:, 1, t:t + 1],
                                                    scale=nr[:, 0, t:t + 1], accum_out=sums[:, 0, t:t + 1])
                    last.then_inc(xn_ok[h], 1)
                    if h == (b == 0) and b + 1 < BATCHES:
                        deviation(b + 1)
                keep_transposes(b, 0)
                if b:
                    act.wait_ge(sq_ok, b)
                sum_squares(b, range(0, TG))
                keep_transposes(b, 1)
                if b == 1:
                    act.wait_ge(pad_ok, CLEARED)
                if b:
                    keep_logits(b - 1)
                if b == 2:
                    act.wait_ge(g1_ps, 1)
                    nc.scalar.activation(g1b1[:], g1p, ACT.Copy)
                    nc.scalar.activation(ws[:], wsp, ACT.Copy).then_inc(g1_ok, 1)
                act.wait_ge(xn_ok[1], b + 1)
                sum_squares(b, range(TG, TB)).then_inc(sq_ok, 1)
                if b == 2:
                    second_deviation(0, 2)
            keep_logits(BATCHES - 1)

            def updates(b):
                for h in range(2):
                    act.wait_ge(q_ok, 2 * b + h + 1)
                    nc.scalar.activation(qe[:, h * TG:(h + 1) * TG, 1:3, R:], shp[h][:, :, 1:3, R:], ACT.Copy).then_inc(e_ok, 1)
                if b == 1:
                    second_deviation(2, BATCHES)
                act.wait_ge(acc_ps, b + 1)
                if b:
                    act.wait_ge(acc_ok, b)
                nc.scalar.activation(macc[:, 0, :, 1:], accp[:, 0, 0:(CB - 1) * 2 * R].rearrange("p (c r) -> p r c", r=2 * R), ACT.Copy)
                nc.scalar.activation(sraw[:, :, 1:], sp_[:, 0:(CB - 1) * 2 * R].rearrange("p (c r) -> p r c", r=2 * R)[:, 0:R, :],
                                     ACT.Copy).then_inc(macc_ok, 1)
                act.wait_ge(acc_ok, b + 1)
                for k in range(KH):
                    nc.scalar.activation(accm[:, k].rearrange("p h (r c) -> p h r c", c=CG),
                                         acc[:, k, 0:R, :].rearrange("p r (h c) -> p h r c", c=CG), ACT.Copy).then_inc(accm_ok, 1)
                nc.scalar.activation(saccm[:].rearrange("p h (r c) -> p h r c", c=CG),
                                     sacc[:].rearrange("p r (h c) -> p h r c", c=CG), ACT.Copy).then_inc(accm_ok, 1)
                for h in range(2):
                    act.wait_ge(at_ps, 2 * b + h + 1)
                    if b:
                        act.wait_ge(cb_ok, b)
                    nc.scalar.activation(sqa[:, h], atp[h], ACT.Square, accum_out=cols[:, 0, h:h + 1]).then_inc(sqa_ok, 1)
                act.wait_ge(nsq_ok, b + 1)
                nc.scalar.activation(cols[:, 3], cols[:, 2], ACT.Sqrt, scale=LR * LR).then_inc(tn_ok, 1)

            for b in range(3):
                updates(b)
            act.wait_ge(beff_ok, 6)
            for g in range(TILES // TG):
                act.wait_ge(xst_ps, g + 1)
                if g < ACT_ALONE:
                    nc.scalar.activation(xst[:, 0, g * GT:(g + 1) * GT], tr[g % SLOTS][:, 0], ACT.Copy)
                nc.scalar.activation(xst[:, 1, g * GT:(g + 1) * GT], tr[g % SLOTS][:, 1], ACT.Copy).then_inc(xst_a, 1)
            with act.Fori(0, ROUNDS) as i:
                for s in range(RING):
                    act.wait_ge(h_ps[s], i + 1)
                    nc.scalar.activation(h_s[0:H, s], hp[s], ACT.Relu, bias=w_s[0:H, s, KH * H:KH * H + 1]).then_inc(h_ok[s], 1)
            updates(3)

        @block.vector
        def _(dve):
            for free in y_out:
                dve.sem_inc(free, CREDIT)
            vec = nc.vector
            n = Count(0)

            def mine(instruction):
                instruction.then_inc(dv, 1)
                dve.wait_ge(dv, n())

            def norm(b):
                for t in range(TB):
                    if t % TG == 0:
                        dve.wait_ge(x_in[2 * b + t // TG], 16)
                    last = vec.bn_stats(stats[:, t], x_all[:, b * TB + t])
                mine(last)
                for t in range(TB):
                    last = vec.bn_aggr(mv[:, t], stats[:, t])
                mine(last)
                vec.tensor_scalar(nrm[:, 0], mv[:, :, 1], EPS, None, ALU.add).then_inc(var_ok, 1)
                dve.wait_ge(dev_ok, b + 1)
                mine(vec.reciprocal(nrm[:, 2], nrm[:, 1]))
                mine(vec.tensor_tensor(nrm[:, 3], nrm[:, 2], nrm[:, 2], ALU.mult))
                mine(vec.tensor_tensor(nrm[:, 3], nrm[:, 3], nrm[:, 0], ALU.mult))
                mine(vec.tensor_scalar(nrm[:, 3], nrm[:, 3], -0.5, 1.5, ALU.mult, ALU.add))
                now = slice(b * TB, (b + 1) * TB)
                mine(vec.tensor_tensor(nr[:, 0, now], nrm[:, 2], nrm[:, 3], ALU.mult))
                vec.scalar_tensor_tensor(nr[:, 1, now], mv[:, :, 0], -1.0, nr[:, 0, now], ALU.mult, ALU.mult).then_inc(nr_ok, 1)

            def choose(b):
                dve.wait_ge(lg_ps, b + 1)
                wide = lambda row: row.unsqueeze(1).broadcast_to([P, TB, E])
                deep = lambda number: number.unsqueeze(2).broadcast_to([P, TB, E])
                vec.tensor_tensor(lg[:, 0], lgp[b % 2][:, :, 0:E], wide(col["rb"]), ALU.add).then_inc(lg_read, 1)
                dve.wait_ge(lg_read, b + 1)
                mine(vec.tensor_reduce(best[:, 0], lg[:, 0], AX.X, ALU.max))
                mine(vec.tensor_tensor(lg[:, 1], lg[:, 0], deep(best[:, 0]), ALU.is_ge))
                mine(vec.tensor_tensor(lg[:, 2], lg[:, 1], wide(edesc), ALU.mult))
                mine(vec.tensor_reduce(best[:, 1], lg[:, 2], AX.X, ALU.max))
                vec.tensor_tensor(oh_all[:, :, b * TB:(b + 1) * TB].rearrange("p e t -> p t e"), lg[:, 2], deep(best[:, 1]),
                                  ALU.is_equal).then_inc(oh_ok, 1)

            def add_base(pairs):
                for q in pairs:
                    dve.wait_ge(base_ps, q + 1)
                    xo = x_all[:, 2 * q:2 * q + 2, :]
                    vec.tensor_tensor(xo, pairp[bank_of(q)], xo, ALU.add).then_inc(base_added, 1)

            def errors(b0, b1):
                tiles, last_one = slice(b0 * TB, b1 * TB), b1 == BATCHES
                wide = lambda v: v[:, tiles].unsqueeze(2).broadcast_to([P, (b1 - b0) * TB, R])
                mean, raw, work, dev = ms[:, tiles, 0], e_raw[:, tiles], tmp_e[:, tiles], ms[:, tiles, 1]
                dve.wait_ge(sq_ok, b1)
                vec.tensor_scalar(mean, sums[:, 0, tiles], 1.0 / D, None, ALU.mult).then_inc(dv, 1)
                vec.tensor_scalar(tmp2[:, 0, tiles], sums[:, 1, tiles], 1.0 / D, EPS, ALU.mult, ALU.add).then_inc(dv, 1)
                dve.wait_ge(dv, n(2))
                mine(vec.tensor_tensor(tmp2[:, 1, tiles], mean, mean, ALU.mult))
                vec.tensor_tensor(tmp2[:, 2, tiles], tmp2[:, 0, tiles], tmp2[:, 1, tiles], ALU.subtract).then_inc(v2_ok, 1)
                dve.wait_ge(sd2_ok, 1 + last_one)
                mine(vec.reciprocal(r2[:, 0, tiles], dev))
                mine(vec.scalar_tensor_tensor(r2[:, 1, tiles], mean, -1.0, r2[:, 0, tiles], ALU.mult, ALU.mult))
                dve.wait_ge(g1_ok, 1)
                dve.wait_ge(ep_ok, b1)
                vec.tensor_tensor(raw, raw, wide(r2[:, 0]), ALU.mult).then_inc(dv, 1)
                vec.tensor_tensor(work, wide(r2[:, 1]), g1b1[:, 0].unsqueeze(1).broadcast_to([P, (b1 - b0) * TB, R]), ALU.mult).then_inc(dv, 1)
                dve.wait_ge(dv, n(2))
                mine(vec.tensor_tensor(work, raw, work, ALU.add))
                vec.tensor_tensor(e_all[:, b0:b1, 0:TB], work.rearrange("p (b t) r -> p b t r", t=TB),
                                  g1b1[:, 1].unsqueeze(1).unsqueeze(1).broadcast_to([P, b1 - b0, TB, R]), ALU.add).then_inc(eb_ok, 1)

            norm(0)
            dve.wait_ge(early_in, 16)
            dve.wait_ge(wa_ps, 1)
            for k in range(KH):
                vec.tensor_scalar(w64[:, k, E:E + R], wa[:, k], gb[:, k, 0:1], None, ALU.mult)
                last = vec.tensor_scalar(bwa[:, k], wa[:, k], gb[:, k, 1:2], None, ALU.mult)
            last.then_inc(w64_ok, 1)
            for b in range(BATCHES):
                if b + 1 < BATCHES:
                    norm(b + 1)
                for h in range(2):
                    dve.wait_ge(tr_ps[h], b + 1)
                    vec.tensor_copy(xt_all[:, 2 * b + h, 0], tr[h][:, 0]).then_inc(xt_ok[h], 1)
                if b:
                    choose(b - 1)
                    add_base((b - 1,))
                if b == 2:
                    errors(0, 2)
            choose(BATCHES - 1)

            carry = reset2[:].rearrange("p a c -> p (a c)")

            def apart(b):
                for h in range(2):
                    dve.wait_ge(sh_ps, 2 * b + h + 1)
                    for g in range(3):
                        t = b * TB + h * TG
                        last = vec.tensor_tensor(qe[:, h * TG:(h + 1) * TG, g, 0:R], shp[h][:, :, g, 0:R],
                                                 r2[:, 0, t:t + TG].unsqueeze(2).broadcast_to([P, TG, R]), ALU.mult)
                    last.then_inc(q_ok, 1)

            def sum_chunks(b):
                dve.wait_ge(acc_ps, b + 1)
                mine(vec.tensor_copy(macc[:, 1, :, 1:], accp[:, 1, 0:(CB - 1) * 2 * R].rearrange("p (c r) -> p r c", r=2 * R)))
                dve.wait_ge(macc_ok, b + 1)
                vec.tensor_tensor_scan(acc.rearrange("p k r c -> p (k r c)"), carry,
                                       macc[:].rearrange("p k r c -> p (k r c)"), 0.0, ALU.mult, ALU.add)
                vec.tensor_tensor_scan(sacc[:].rearrange("p r c -> p (r c)"), carry[0:2, 0:R * CB],
                                       sraw[:].rearrange("p r c -> p (r c)"), 0.0, ALU.mult, ALU.add).then_inc(acc_ok, 1)
                dve.wait_ge(acc_ok, b + 1)
                for h in range(2):
                    for k in range(KH):
                        v = acc[:, k, R:, h * CG:(h + 1) * CG]
                        last = vec.tensor_tensor(sqb[:, h, k].rearrange("p (r c) -> p r c", c=CG), v, v, ALU.mult)
                last.then_inc(sqb_ok, 1)

            def mask(b, h):
                dve.wait_ge(mid_ps, 2 * b + h + 1)
                vec.tensor_tensor(midm[:, h], midp[b < EARLY_BASE][h], diag, ALU.mult).then_inc(mid_ok, 1)

            def add_up(b, h):
                if b >= 2:
                    for t in range(b * TB + h * TG, b * TB + (h + 1) * TG):
                        dve.wait_ge(*gathered(t))
                dve.wait_ge(o_ps[h], b + 1)
                for q in range(TG // 2):
                    t = h * TG + 2 * q
                    xo = x_all[:, b * TB + t:b * TB + t + 2, :]
                    last = vec.tensor_tensor(xo, ps[:, 4 + t // 2, :].rearrange("p (t d) -> p t d", t=2), xo, ALU.add)
                last.then_inc(o_read[h], 1)

            def norms(b):
                dve.wait_ge(cb_ps, b + 1)
                dve.wait_ge(sqa_ok, 2 * b + 2)
                vec.tensor_tensor(cols[:, 1], cbp, cols[:, 0], ALU.add).then_inc(cb_ok, 1)
                dve.wait_ge(nsq_ps, b + 1)
                vec.tensor_scalar(cols[:, 2], nsqp, 1e-30, None, ALU.max).then_inc(nsq_ok, 1)
                dve.wait_ge(tn_ok, b + 1)
                mine(vec.tensor_scalar(cols[:, 4], cols[:, 3], 1e-6, None, ALU.add))
                mine(vec.reciprocal(cols[:, 5], cols[:, 4]))
                mine(vec.tensor_scalar(cols[:, 4], cols[:, 5], 1.0, -LR, ALU.min, ALU.mult))
                mine(vec.tensor_scalar(cols[:, 5], cols[:, 4], SCALING, None, ALU.mult))
                for h in range(2):
                    vec.tensor_scalar(dnb[:, h], ident, cols[:, 4, h:h + 1], None, ALU.mult)
                for h in range(2):
                    last = vec.scalar_tensor_tensor(aeff[:, b % 2, h], atp[h], cols[:, 5, h:h + 1], at2[:], ALU.mult, ALU.add)
                last.then_inc(aeff_ok, 1)

            def clipped_b(b):
                for h in range(2):
                    dve.wait_ge(nb_ps, 2 * b + h + 1)
                    for k in range(KH):
                        vec.tensor_tensor(beff[:, h, k].rearrange("p (r c) -> p r c", c=CG), acc[:, k, R:, h * CG:(h + 1) * CG],
                                          nbp[h].rearrange("p (r c) -> p r c", c=CG), ALU.mult).then_inc(dv, 1)
                    dve.wait_ge(dv, n(2))
                    vec.tensor_tensor(beff[:, h], beff[:, h], btrep, ALU.add).then_inc(beff_ok, 1)

            def step(b):
                apart(b)
                if b < EARLY_BASE:
                    add_base((TB + b - 1,))
                if b == 1:
                    errors(2, BATCHES)
                sum_chunks(b)
                mask(b - 1, 0)
                mask(b - 1, 1)
                norms(b)
                add_up(b - 1, 0)
                clipped_b(b)
                add_up(b - 1, 1)

            apart(0)
            flat = lambda t: t.rearrange("p e t -> p (e t)")
            dve.wait_ge(rank_ps, 1)
            mine(vec.tensor_tensor_scan(flat(cin[:]), flat(reset[:]), total, 0.0, ALU.mult, ALU.add))
            vec.tensor_tensor(flat(place[:]), rank, flat(cin[:]), ALU.add).then_inc(counted, 1)
            dve.wait_ge(counted, 1)
            tiles, cn, ct, off, dist, pack, cmp, sel, found = (rt[:, i] for i in range(9))
            num = cin[:, :, TILES - 1]
            mine(vec.tensor_scalar(qi[:], num, float(P - 1), None, ALU.add))
            mine(vec.tensor_scalar(qi[:], qi[:], 7, 7, ALU.arith_shift_right, ALU.logical_shift_left))
            mine(vec.tensor_copy(tiles, qi[:]))
            always = col["ones"][:, 0:E]
            vec.tensor_tensor_scan(cn, always, num, 0.0, ALU.mult, ALU.add).then_inc(dv, 1)
            vec.tensor_tensor_scan(ct, always, tiles, 0.0, ALU.mult, ALU.add).then_inc(dv, 1)
            dve.wait_ge(dv, n(2))
            mine(vec.tensor_tensor(off, cn, num, ALU.subtract))
            mine(vec.tensor_tensor(dist, ct, tiles, ALU.subtract))
            mine(vec.tensor_tensor(dist, dist, off, ALU.subtract))
            mine(vec.scalar_tensor_tensor(pack, dist, float(PK), off, ALU.mult, ALU.add))
            mine(vec.tensor_tensor(place[:], place[:], pack.unsqueeze(2).broadcast_to([P, E, TILES]), ALU.add))
            mine(vec.tensor_tensor(place[:], place[:], oh_all[:], ALU.mult))
            mine(vec.tensor_reduce(found, place[:].rearrange("p e t -> p t e"), AX.X, ALU.add))
            mine(vec.tensor_copy(vi[:, 0], found))
            vec.tensor_scalar(vi[:, 1], vi[:, 0], PK - 1, None, ALU.bitwise_and).then_inc(place_ok, 1)
            vec.tensor_scalar(vi[:, 2], vi[:, 0], 12, None, ALU.arith_shift_right).then_inc(dv, 1)
            dve.wait_ge(dv, n())
            dve.wait_ge(place_ok, 1)
            vec.tensor_tensor(vi[:, 3], vi[:, 1], vi[:, 2], ALU.add)
            sum_chunks(0)
            add_base(range(3, 6))
            norms(0)
            add_base(range(6, 7))
            clipped_b(0)
            mine(vec.tensor_scalar(cmp, ct, icol, None, ALU.is_le))
            mine(vec.tensor_reduce(item[:, 2:3], cmp, AX.X, ALU.add))
            mine(vec.tensor_scalar(item[:, 0:1], item[:, 2:3], float(E - 1), None, ALU.min))
            mine(vec.scalar_tensor_tensor(sel, eiota, item[:, 0:1], dist, ALU.is_equal, ALU.mult))
            mine(vec.tensor_reduce(item[:, 3:4], sel, AX.X, ALU.add))
            mine(vec.tensor_tensor(item[:, 2:3], icol, item[:, 3:4], ALU.subtract))
            vec.tensor_scalar(item[:, 1:2], item[:, 2:3], float(N), None, ALU.min).then_inc(item_ok, 1)
            add_base(range(7, 8))
            dve.wait_ge(item_ps, 1)
            vec.tensor_copy(item_row[:], rowp).then_inc(row_ok, 1)
            step(1)
            step(2)
            add_base(range(10, 12))
            for g in range(ACT_ALONE, TILES // TG):
                dve.wait_ge(xst_ps, g + 1)
                vec.tensor_copy(xst[:, 0, g * GT:(g + 1) * GT], tr[g % SLOTS][:, 0]).then_inc(xst_v, 1)
            with dve.Fori(0, ROUNDS) as i:
                for s in range(RING):
                    dve.wait_ge(y_ps[s], CREDIT + i + 1)
                    if s % HALF == 0:
                        dve.wait_ge(y_out[s // HALF], CREDIT + 16 * i)
                    vec.tensor_scalar(y_s[:, s], yp[s], 0.0, None, ALU.max).then_inc(y_ok[s], 1)
            step(3)
            mask(3, 0)
            add_up(3, 0)
            mask(3, 1)
            add_up(3, 1)

        @block.tensor
        def _(pe):
            mm = nc.tensor.matmul
            pe.wait_ge(early_in, 16)
            for m in range(KH):
                for k in range(KH):
                    last = mm(wa[:, m], wp[:, k, m * P:(m + 1) * P], a_w[:, k], start=(k == 0), stop=(k == KH - 1))
            last.then_inc(wa_ps, 1)

            def transpose_group(s, rows, done):
                for t in range(TG):
                    for k in range(KH):
                        last = nc.tensor.transpose(tr[s][:, k, t * P:(t + 1) * P], rows[:, t, k * P:(k + 1) * P], ident)
                last.then_inc(done, 1)

            def shifts(b):
                pe.wait_ge(eb_ok, 1 + b // 2)
                if b:
                    pe.wait_ge(aeff_ok, b)
                for h in range(2):
                    t0, t1 = h * TG, (h + 1) * TG
                    p_b, e_b = p_all[:, b], e_all[:, b]
                    mm(shp[h][:, :, 0, 0:R], shift[0], p_b[:, t0:t1], start=True, stop=False)
                    mm(shp[h][:, :, 1, 0:R], shift[1], p_b[:, t0 + 1:t1 + 1], start=False, stop=False)
                    mm(shp[h][:, :, 2, 0:R], shift[2], p_b[:, t0 + 1:t1 + 1], start=False, stop=False)
                    mm(shp[h][:, :, 1, R:], shift[3], e_b[:, t0:t1], start=False, stop=False)
                    mm(shp[h][:, :, 2, R:], shift[4], e_b[:, t0:t1], start=False, stop=False)
                    mm(shp[h][:, :, 2, R:], shift[5], e_b[:, t0 + 1:t1 + 1], start=False, stop=True).then_inc(sh_ps, 1)

            def early_base(pairs):
                for q in pairs:
                    if q > TB:
                        pe.wait_ge(o_read[0], (q - TB + 2) // 2)
                    elif q == STAGE_1_PAIRS:
                        pe.wait_ge(counted, 1)
                        pe.wait_ge(base_added, q)
                    elif q >= STAGE_1_PAIRS + 4:
                        pe.wait_ge(base_added, q - 3)
                    elif 0 < q < STAGE_1_PAIRS:
                        pe.wait_ge(base_added, q)
                    for t in range(2 * q, 2 * q + 2):
                        for k in range(KH):
                            last = mm(pairp[bank_of(q)][:, t % 2], xt_all[:, t // TG, k, (t % TG) * P:(t % TG + 1) * P], wbt[:, k],
                                      start=(k == 0), stop=(k == KH - 1))
                    last.then_inc(base_ps, 1)

            for b in range(BATCHES):
                for h in range(2):
                    pe.wait_ge(xn_ok[h], b + 1)
                    if b:
                        pe.wait_ge(xt_ok[h], 2 * b)
                    transpose_group(h, xn_all[:, b * TB + h * TG:b * TB + (h + 1) * TG], tr_ps[h])
                pe.wait_ge(w64_ok, 1)
                if b > 1:
                    pe.wait_ge(ep_ok, b - 1)
                if b == 2:
                    pe.wait_ge(made_ok, MADE)
                    for k in range(KH):
                        mm(g1p[:, 0], ones, w64[:, k, E:E + R], start=(k == 0), stop=(k == KH - 1))
                    for k in range(KH):
                        mm(g1p[:, 1], ones, bwa[:, k], start=(k == 0), stop=(k == KH - 1))
                    for k in range(KH):
                        last = mm(wsp, gbn[:, k], wpt[:, k], start=(k == 0), stop=(k == KH - 1))
                    last.then_inc(g1_ps, 1)
                for h in range(2):
                    pe.wait_ge(xt_ok[h], 2 * b + 2)
                    for t in range(TG):
                        for k in range(KH):
                            last = mm(lgp[b % 2][:, h * TG + t], xt_all[:, 2 * b + h, k, t * P:(t + 1) * P], w64[:, k], start=(k == 0), stop=(k == KH - 1))
                last.then_inc(lg_ps, 1)
                if b < STAGE_1_PAIRS:
                    pe.wait_ge(late_in, 16)
                    early_base((b,))
            pe.wait_ge(pad_ok, CLEARED)
            shifts(0)
            pe.wait_ge(oh_ok, BATCHES)
            pe.wait_ge(ep_ok, BATCHES)
            pe.wait_ge(g1_ok, 1)
            oh = oh_all[:].rearrange("p e t -> p (e t)")
            for c in range(2):
                mm(total[:, c * 512:(c + 1) * 512], ones_bf[:], oh[:, c * 512:(c + 1) * 512], start=True, stop=True)
            for c in range(2):
                last = mm(rank[:, c * 512:(c + 1) * 512], ntri_bf[:], oh[:, c * 512:(c + 1) * 512], start=True, stop=True)
            last.then_inc(rank_ps, 1)

            def sums_of_chunks(b):
                if b:
                    pe.wait_ge(beff_ok, 2 * b)
                for k in range(KH):
                    mm(accp[:, k], zero[:, 0:P], zero[:, 0:512], start=True, stop=False)
                pe.wait_ge(q_ok, 2 * b + 2)
                pe.wait_ge(e_ok, 2 * b + 2)
                mm(sp_, zero[:, 0:2], zero[:, 0:512], start=True, stop=False)
                for t in range(TB):
                    g = 1 if t == 0 else 0
                    rhs = qe[:, t, g:]
                    cols_ = slice((2 * t - 1 + g) * 2 * R, (2 * t + 2) * 2 * R)
                    for k in range(KH):
                        mm(accp[:, k, cols_], xn_all[:, b * TB + t, k * P:(k + 1) * P], rhs, start=False, stop=(t == TB - 1))
                    last = mm(sp_[:, cols_], ms[:, b * TB + t], rhs, start=False, stop=(t == TB - 1))
                last.then_inc(acc_ps, 1)

            def updates_of_a(b):
                for h in range(2):
                    for k in range(KH):
                        if h == 0:
                            pe.wait_ge(accm_ok, (KH + 1) * b + k + 1)
                        mm(atp[h], accm[:, k, h], wpgt[:, k], start=(k == 0), stop=False)
                    if h == 0:
                        pe.wait_ge(accm_ok, (KH + 1) * (b + 1))
                    mm(atp[h], saccm[:, h], ws[:], start=False, stop=True).then_inc(at_ps, 1)

            def squares_of_b(b):
                pe.wait_ge(sqb_ok, b + 1)
                pe.wait_ge(sqa_ok, 2 * b + 2)
                for h in range(2):
                    for k in range(KH):
                        last = mm(cbp[:, h:h + 1], sqb[:, h, k], ones[:, 0:1], start=(k == 0), stop=(k == KH - 1))
                last.then_inc(cb_ps, 1)

            def base(b, tiles):
                for t in tiles:
                    h = t // TG
                    if t % TG == 0:
                        pe.wait_ge(o_read[h], b)
                    for k in range(KH):
                        mm(op[t], xt_all[:, 2 * b + h, k, (t % TG) * P:(t % TG + 1) * P], wbt[:, k], start=(k == 0 and t % 2 == 0), stop=False)

            def mid(b, halves=range(2)):
                for h in halves:
                    if h == 0 and b == 0:
                        pe.wait_ge(base_added, TB)
                        pe.wait_ge(row_ok, 1)
                    if h == 0 and 0 < b < EARLY_BASE:
                        pe.wait_ge(o_read[1], b)
                    pe.wait_ge(beff_ok, 2 * b + h + 1)
                    for k in range(KH):
                        last = mm(midp[b < EARLY_BASE][h], beff[:, h, k], xt_all[:, 2 * b + h, k], start=(k == 0), stop=(k == KH - 1))
                    last.then_inc(mid_ps, 1)

            def lora(b, tiles):
                for t in tiles:
                    h = t // TG
                    if t % TG == 0:
                        pe.wait_ge(mid_ok, 2 * b + h + 1)
                        if h == 0 and b < EARLY_BASE - 1:
                            pe.wait_ge(base_added, TB + b + 1)
                        if 0 < b < EARLY_BASE:
                            pe.wait_ge(o_read[h], b)
                    last = mm(op[t], midm[:, h, (t % TG) * P:(t % TG + 1) * P], aeff[:, b % 2, h],
                              start=(b < EARLY_BASE and t % 2 == 0), stop=(t % 2 == 1))
                    if t % TG == TG - 1:
                        last.then_inc(o_ps[h], 1)

            def common_factor(b):
                pe.wait_ge(cb_ok, b + 1)
                mm(nsqp, blk, cols[:, 1], start=True, stop=True).then_inc(nsq_ps, 1)

            def factors_of_b(b):
                pe.wait_ge(aeff_ok, b + 1)
                for h in range(2):
                    mm(nbp[h], ones, dnb[:, h], start=True, stop=True).then_inc(nb_ps, 1)

            sums_of_chunks(0)
            early_base(range(3, 6))
            updates_of_a(0)
            early_base(range(6, 7))
            squares_of_b(0)
            common_factor(0)
            early_base(range(7, 8))
            factors_of_b(0)
            early_base(range(8, 9))
            pe.wait_ge(item_ok, 1)
            pe.wait_ge(base_added, 7)
            for c in range(2):
                last = nc.tensor.transpose(rowp[:, c * P:(c + 1) * P], item[:, c:c + 1], ident)
            last.then_inc(item_ps, 1)
            def step(b):
                shifts(b)
                sums_of_chunks(b)
                mid(b - 1)
                updates_of_a(b)
                lora(b - 1, range(0, 2))
                squares_of_b(b)
                lora(b - 1, range(2, 4))
                common_factor(b)
                lora(b - 1, range(4, 8))
                factors_of_b(b)

            step(1)
            early_base(range(9, 10))
            step(2)
            early_base(range(10, 12))

            left_by = [(aeff_ok, 3), (beff_ok, 6), (base_added, 12), (o_read[1], 2)]
            for g in range(TILES // TG):
                if g < SLOTS:
                    pe.wait_ge(*left_by[g])
                else:
                    pe.wait_ge(xst_a, g - SLOTS + 1)
                    if g - SLOTS >= ACT_ALONE:
                        pe.wait_ge(xst_v, g - SLOTS + 1 - ACT_ALONE)
                pe.wait_ge(xs_in[g], 16)
                transpose_group(g % SLOTS, xs_s[:, g % ROOMS], xst_ps)
            pe.wait_ge(xst_a, TILES // TG)
            pe.wait_ge(xst_v, TILES // TG - ACT_ALONE)
            pe.wait_ge(pad_ok, CLEARED + 1)

            def first_tokens(i, s, count):
                _, values = nc.values_load_multi_w_load_instructions(
                    item_row[0:1, bass.ds(P + i * RING + s, count)], engines=[mybir.EngineType.PE], min_val=0, max_val=N,
                    skip_runtime_bounds_check_because="the routing's minimum with N bounds them")
                return values

            def first_layer(i, s, first_token):
                pe.wait_ge(w_in[s], 16 * (i + 1))
                for k in range(KH):
                    last = mm(hp[s], w_s[:, s, k * H:(k + 1) * H], xst[:, k, bass.ds(first_token, P)], start=(k == 0), stop=(k == KH - 1))
                last.then_inc(h_ps[s], 1)

            def second_layer(i, s):
                pe.wait_ge(h_ok[s], i + 1)
                if s % 2 == 0:
                    if s < BANKS:
                        pe.wait_ge(y_ok[s + 1 + BANKS], CREDIT + i)
                    else:
                        pe.wait_ge(y_ok[s + 1 - BANKS], CREDIT + i + 1)
                mm(yp[s], h_s[:, s], w_s[0:H + 1, s, KH * H + 1:], start=True, stop=True).then_inc(y_ps[s], 1)

            AHEAD = 2
            tokens = first_tokens(0, 0, AHEAD)
            for s in range(AHEAD):
                first_layer(0, s, tokens[s])

            def one_round(i, last):
                tokens = first_tokens(i, AHEAD, RING - AHEAD if last else RING)
                for s in range(RING):
                    ahead = s + AHEAD
                    if ahead < RING:
                        first_layer(i, ahead, tokens[s])
                    elif not last:
                        first_layer(i + 1, ahead - RING, tokens[s])
                    second_layer(i, s)

            with pe.Fori(0, ROUNDS - 1) as i:
                one_round(i, False)
            one_round(ROUNDS - 1, True)
            for s in range(BANKS, RING):
                pe.wait_ge(y_ok[s], CREDIT + ROUNDS)
            step(3)
            base(3, range(0, 4))
            mid(3, range(0, 1))
            base(3, range(4, 8))
            lora(3, range(0, 4))
            mid(3, range(1, 2))
            lora(3, range(4, 8))


def kernel(L0_attn_x, L0_attn_Wb, L0_attn_init_A, L0_attn_init_B, L0_attn_ln_gamma, L0_attn_ln_beta, L0_attn_Wp,
           L0_ffn_router_w, L0_ffn_router_b, L0_ffn_weights1, L0_ffn_bias1, L0_ffn_weights2, L0_ffn_bias2):
    import numpy as np
    import concourse.bacc as bacc
    from concourse.bass_utils import run_bass_kernel_spmd

    f = lambda a: np.ascontiguousarray(np.asarray(a))
    halves = lambda a: f(a).reshape(KH, P, -1).transpose(1, 0, 2).reshape(P, -1)
    eye = np.eye(P, dtype=np.float32)
    k, m = np.arange(P)[:, None], np.arange(P)[None, :]
    shifts = [(k == P - 1) & (m == 0), (k == m - 1) & (m <= CHUNK), (k == m - 1) & (m > CHUNK),
              (k == m + 1) & (m < CHUNK), (k == m + 1) & (m >= CHUNK), (k == 0) & (m == P - 1)]
    router, b_t = f(L0_ffn_router_w).T, f(L0_attn_init_B).T
    parts = {
        "ident": eye,
        "w64": halves(np.concatenate([router, np.zeros((D, R), np.float32), b_t], 1)),
        "rb": np.tile(f(L0_ffn_router_b), (P, 1)),
        "edesc": np.tile(E - np.arange(E), (P, 1)),
        "wp": halves(L0_attn_Wp),
        "a": halves(L0_attn_init_A),
        "gb": halves(np.stack([f(L0_attn_ln_gamma), f(L0_attn_ln_beta)], 1)),
        "eiota": np.tile(np.arange(E), (P, 1)),
        "icol": P * np.arange(P)[:, None],
        "ones": np.ones((P, P)),
        "ntri": -1.0 * (k >= m),
        "sh": np.concatenate(shifts, 1),
        "blk": k % CG == m % CG,
        "diag": k % CG == np.arange(GT)[None, :] // CHUNK,
        "wpt": halves(f(L0_attn_Wp).T),
        "wbt": halves(f(L0_attn_Wb).T),
        "atrep": np.repeat(f(L0_attn_init_A).T, CG, 0),
        "btrep": halves(np.repeat(b_t, CG, 1)),
    }
    pack = lambda names: np.concatenate([parts[n].astype(np.float32) for n, _ in names], 1)
    w1 = f(L0_ffn_weights1).reshape(E, KH, P, H).transpose(0, 2, 1, 3).reshape(E, P, KH * H)
    below = lambda parts: np.concatenate([*parts, np.zeros((E, P - sum(p.shape[1] for p in parts), parts[0].shape[2]), np.float32)], 1)
    b1 = below([f(L0_ffn_bias1)[:, :, None]])
    w2 = below([f(L0_ffn_weights2), f(L0_ffn_bias2)[:, None, :]])
    arrays = {"x": f(L0_attn_x).reshape(N, D), "early": pack(EARLY), "late": pack(LATE), "wx": np.concatenate([w1, b1, w2], 2)}
    nc = bacc.Bacc("TRN2", target_bir_lowering=False, num_devices=1)
    args = [nc.dram_tensor(n, list(a.shape), F32, kind="ExternalInput").ap() for n, a in arrays.items()]
    out = nc.dram_tensor("out", [N, D], F32, kind="ExternalOutput").ap()
    build(nc, *args, out)
    got = run_bass_kernel_spmd(nc, [{n: np.ascontiguousarray(a) for n, a in arrays.items()}], core_ids=[0])
    return got.results[0]["out"].reshape(L0_attn_x.shape)
```
